# Optimizing a Trainium2 kernel written in Bass

```python
import numpy as np
import jax
import jax.numpy as jnp

def _softmax(x, axis=-1):
    return jax.nn.softmax(x, axis=axis)

def _gelu(x):
    return jax.nn.gelu(x, approximate=True)

def _silu(x):
    return jax.nn.silu(x)

def _sigmoid(x):
    return jax.nn.sigmoid(x)

def _layernorm(x, axis=-1, eps=1e-05):
    m = jnp.mean(x, axis=axis, keepdims=True)
    v = jnp.var(x, axis=axis, keepdims=True)
    return (x - m) / jnp.sqrt(v + eps)

def _scatter_add(tgt, idx, src, axis=0):
    return tgt.at[idx].add(src)

def _segment_sum(src, seg, n):
    return jax.ops.segment_sum(src, seg, n)
kernel_name = 'mk_cond_resid_d2_seqx_r8_94d367'

def setup_inputs(seed: int=0):
    np.random.seed(seed)
    _w = jnp.asarray

    def _rec_inputs():
        import jax
        import jax.numpy as jnp
        _rk = jax.random.key(seed)
        x = 7.22e-05 + 1 * jax.random.normal(jax.random.fold_in(_rk, 1), (8, 128, 256), jnp.float32)
        _lenS = 128 - jax.random.randint(jax.random.fold_in(_rk, 7), (8,), 0, max(1, 128 // 4) + 1, jnp.int32)
        _lenS2 = 128 - jax.random.randint(jax.random.fold_in(_rk, 8), (8,), 0, max(1, 128 // 4) + 1, jnp.int32)
        cond_2048 = jax.random.bernoulli(jax.random.fold_in(_rk, 11), 0.8975, (8, 256)).astype(jnp.float32)
        return (x, cond_2048)
    x, cond_2048 = _rec_inputs()

    def _L0_cond_setup():
        import jax, jax.numpy as jnp
        import numpy as np
        import math
        D_MODEL = 128
        NUM_HEAD = 16
        NEG_INF = -1e+30
        key = jax.random.key(seed)
        k_x, k_m, k_q, k_k, k_v = jax.random.split(key, 5)
        B, C, T = (4, D_MODEL, 256)
        x = jax.random.normal(k_x, (B, C, T), dtype=jnp.float32)
        mask = (jax.random.uniform(k_m, (B, T)) < 0.9).astype(jnp.float32)
        limit = math.sqrt(6.0 / (C + C))
        Wq = jax.random.uniform(k_q, (C, C), minval=-limit, maxval=limit, dtype=jnp.float32)
        Wk = jax.random.uniform(k_k, (C, C), minval=-limit, maxval=limit, dtype=jnp.float32)
        Wv = jax.random.uniform(k_v, (C, C), minval=-limit, maxval=limit, dtype=jnp.float32)
        b = jnp.zeros((1,), dtype=jnp.float32)
        return {'x': x, 'mask': mask, 'Wq': Wq, 'Wk': Wk, 'Wv': Wv, 'b': b}
    _L0_cond_all = _L0_cond_setup()
    _L0_cond_in = {k: v for k, v in _L0_cond_all.items() if k in ('Wq', 'Wk', 'Wv', 'b')}
    del _L0_cond_all

    def _L1_cond_setup():
        import jax, jax.numpy as jnp
        import numpy as np
        B, T, D = (16, 128, 256)
        key = jax.random.key(seed)
        k0, k1, k2, k3 = jax.random.split(key, 4)
        scale = 1.0 / np.sqrt(D)
        return {'initial_state': jax.random.normal(k0, (B, D), jnp.float32), 'inputs': jax.random.normal(k1, (B, T, D), jnp.float32), 'W_ih': jax.random.normal(k2, (D, 3 * D), jnp.float32) * scale, 'W_hh': jax.random.normal(k3, (D, 3 * D), jnp.float32) * scale, 'b_ih': jnp.zeros((3 * D,), jnp.float32), 'b_hh': jnp.zeros((3 * D,), jnp.float32)}
    _L1_cond_all = _L1_cond_setup()
    _L1_cond_in = {k: v for k, v in _L1_cond_all.items() if k in ('W_ih', 'W_hh', 'b_ih', 'b_hh')}
    del _L1_cond_all
    return {'x': x, 'cond_2048': cond_2048, 'L0_cond_Wq': _L0_cond_in['Wq'], 'L0_cond_Wk': _L0_cond_in['Wk'], 'L0_cond_Wv': _L0_cond_in['Wv'], 'L0_cond_b': _L0_cond_in['b'], 'L1_cond_W_ih': _L1_cond_in['W_ih'], 'L1_cond_W_hh': _L1_cond_in['W_hh'], 'L1_cond_b_ih': _L1_cond_in['b_ih'], 'L1_cond_b_hh': _L1_cond_in['b_hh']}

def reference(x, cond_2048, L0_cond_Wq, L0_cond_Wk, L0_cond_Wv, L0_cond_b, L1_cond_W_ih, L1_cond_W_hh, L1_cond_b_ih, L1_cond_b_hh):
    import jax
    import jax.numpy as jnp

    def _L0_cond_ref(x, mask, Wq, Wk, Wv, b):
        import jax, jax.numpy as jnp
        import numpy as np
        import math
        D_MODEL = 128
        NUM_HEAD = 16
        NEG_INF = -1e+30
        B, C, T = x.shape
        H = NUM_HEAD
        Dh = C // H

        def proj(W):
            y = jnp.einsum('oc,bct->bto', W, x)
            return y.reshape(B, T, H, Dh).transpose(0, 2, 1, 3)
        Q, K, V = (proj(Wq), proj(Wk), proj(Wv))
        att = jnp.einsum('bhqd,bhkd->bhqk', Q, K) * (1.0 / math.sqrt(Dh))
        att = att + b[0]
        m = mask[:, None, None, :]
        att = att * m + (1.0 - m) * NEG_INF
        att = jax.nn.softmax(att, axis=-1)
        y = jnp.einsum('bhqk,bhkd->bhqd', att, V)
        y = y.transpose(0, 2, 1, 3).reshape(B, T, C)
        return y.transpose(0, 2, 1)

    def _L1_cond_ref(initial_state, inputs, W_ih, W_hh, b_ih, b_hh):
        import jax, jax.numpy as jnp
        import numpy as np
        B, T, D = (16, 128, 256)
        "ScanOverTime(GRU cell): sequential per-timestep module call with\n            dict-state passing; merge_dict_trees stacks the per-step\n            'state_predicted' tensors along axis=1 -> [B, T, D]."

        def cell(h, x):
            gi = x @ W_ih + b_ih
            gh = h @ W_hh + b_hh
            i_r, i_z, i_n = jnp.split(gi, 3, axis=-1)
            h_r, h_z, h_n = jnp.split(gh, 3, axis=-1)
            r = jax.nn.sigmoid(i_r + h_r)
            z = jax.nn.sigmoid(i_z + h_z)
            n = jnp.tanh(i_n + r * h_n)
            h_new = (1.0 - z) * n + z * h
            return (h_new, h_new)
        xs = jnp.swapaxes(inputs, 0, 1)
        _, hs = jax.lax.scan(cell, initial_state, xs)
        return jnp.swapaxes(hs, 0, 1)
    x = x + _L0_cond_ref(x, cond_2048, L0_cond_Wq, L0_cond_Wk, L0_cond_Wv, L0_cond_b)
    x = x + _L1_cond_ref(cond_2048, x, L1_cond_W_ih, L1_cond_W_hh, L1_cond_b_ih, L1_cond_b_hh)
    return x

_drawn_inputs = setup_inputs


def setup_inputs(seed=0):
    import zlib

    import numpy as np

    out = dict(_drawn_inputs(seed))
    spreads = {'L1_cond_b_ih': (0.0, 0.1), 'L1_cond_b_hh': (0.0, 0.1)}
    factors = {}
    for name, (base, spread) in spreads.items():
        noise = np.random.default_rng([zlib.crc32(name.encode()), seed]).standard_normal(out[name].shape)
        drawn = base * np.exp(spread * noise) if base else spread * noise
        out[name] = jnp.asarray(drawn.astype(out[name].dtype))
    for name, factor in factors.items():
        out[name] = (out[name] * factor).astype(out[name].dtype)
    return out
```

```python
from contextlib import ExitStack

import concourse.bass as bass
from concourse import mybir

F32 = mybir.dt.float32
BF16 = mybir.dt.bfloat16
ACT = mybir.ActivationFunctionType
ALU = mybir.AluOpType
AX = mybir.AxisListType

B = 8
C = 128
T = 256
H = 16
DH = C // H
NI = T // 128
NJ = 4
W64 = T // NJ
BT = B * T
OCT = 8
ITER = 2 * OCT
STEPS = C
GRP = 4
EXT = DH + 1
LEAD_MAX, LEAD_ROW, LEAD_EXP = 5, 4, 3
TERMS = 6 * DH
ROW_T = 32
ROW_M = ROW_T + TERMS
NROW = ROW_M + 3
SCALE = float(DH) ** -0.5
NEG = -1e30 / SCALE


def live(n, end):
    return not isinstance(n, int) or 0 <= n < end


def at_least(eng, sem, n, most=1 << 20):
    if isinstance(n, int):
        if n <= 0:
            return
        n = min(n, most)
    eng.wait_ge(sem, n)


def build(nc, x, mask, Wq, Wk, Wv, att_b, W_ih, W_hh, b_ih, b_hh, out):
    with ExitStack() as ctx:
        def sb(name, shape, dt=F32):
            return ctx.enter_context(nc.sbuf_tensor(name, shape, dt))

        def bank(name):
            return ctx.enter_context(nc.psum_tensor(name, [128, 512], F32))

        def sem(name):
            return ctx.enter_context(nc.semaphore(name))

        q_dram = nc.dram_tensor("q_pieces", [3, C, BT], BF16).ap()
        k_dram = nc.dram_tensor("k_pieces", [3, C, BT], BF16).ap()
        row_dram = nc.dram_tensor("mask_rows", [6, BT], BF16).ap()

        x_sb = sb("x_sb", [C, BT])
        xp = sb("xp", [C, BT])
        mask_bc = sb("mask_bc", [C, BT])
        w_nat = sb("w_nat", [C, 3, C])
        wT = sb("wT", [C, 3, C])
        wih = sb("wih", [128, NI, 3 * T])
        wih_n = sb("wih_n", [128, NI, NI, 128])
        whh = sb("whh", [128, NI, 3 * T])
        bih_bc = sb("bih_bc", [128, 3 * T])
        bhh_bc = sb("bhh_bc", [128, 3 * T])
        bias_gi = sb("bias_gi", [128, NJ, 2, W64])
        bias_n = sb("bias_n", [128, NI])
        bhn_p = sb("bhn_p", [128, 3, T], BF16)
        bhn_r = sb("bhn_r", [128, 2, T])
        bhn_rows = sb("bhn_rows", [128, T], BF16)
        ones_rows = sb("ones_rows", [128, 32], BF16)
        ident = sb("ident", [128, 128])
        identb = sb("identb", [128, 128], BF16)
        sel = sb("sel", [128, ITER, 32])
        mask8 = sb("mask8", [B, T])
        m8 = sb("m8", [B, 4, T])
        m8s = sb("m8s", [B, 4])
        rows8 = sb("rows8", [B, 6, T], BF16)
        q_p = sb("q_p", [C, 3, BT], BF16)
        k_p = sb("k_p", [C, 3, BT], BF16)
        q_rest = sb("q_rest", [C, BT])
        k_msk = sb("k_msk", [C, BT])
        k_rest = sb("k_rest", [C, BT])
        v_all = sb("v_all", [128, H, B * NI, EXT])
        xT = sb("xT", [128, NI, C, B])

        stk1 = [[sb(f"{n}max{par}", [128, BT], BF16) for n in "qk"] for par in range(2)]
        stk2 = [[sb(f"{n}exp{par}", [128, BT], BF16) for n in "qk"] for par in range(2)]
        neg_max = sb("neg_max", [128, 2, B * NI])
        mx_p = sb("mx_p", [128, 8, B * NI], BF16)
        mx_r = sb("mx_r", [128, 2, B * NI])
        zero16 = sb("zero16", [128, NI * B])
        half16 = sb("half16", [128, NI * B])
        carrier = sb("carrier", [128, 1])
        mx_rows = sb("mx_rows", [3 * B * NI, 128], BF16)
        v_cur = sb("v_cur", [128, B * NI, 32])
        probs = sb("probs", [128, 2, GRP, NI * T])
        yT = sb("yT", [128, T])
        y_inv = sb("y_inv", [128, NI, GRP])
        y_n = sb("y_n", [128, NI, GRP, DH])
        x1_cur = sb("x1_cur", [128, NI, 2, DH, B])
        gi_next = sb("gi_next", [128, NJ, 2 * W64])
        gi_cur = sb("gi_cur", [128, NJ, 2 * W64])
        gin_cur = sb("gin_cur", [128, NI, ITER, B])

        h0 = sb("h0", [128, W64])
        h0T = sb("h0T", [128, NI, 32])
        tr = sb("tr", [128, W64])
        tz = sb("tz", [128, W64])
        tzT = sb("tzT", [128, NI, 32])
        hh = sb("hh", [128, NI * B])
        n_mul = sb("n_mul", [128, NI, 32, 2])
        n_add = sb("n_add", [128, NI, 32, 2])
        n_pre = sb("n_pre", [128, NI, 32, 2])
        h_mul = sb("h_mul", [128, NI * B, 2])
        h_add = sb("h_add", [128, NI * B, 2])
        h_st = sb("h_st", [128, NI * B, 2])
        oT = sb("oT", [128, 2, NI, 128])
        o_sb = sb("o_sb", [128, 2, T])

        bN, bZ = bank("bN"), bank("bZ")
        bS1, bS2 = bank("bS1"), bank("bS2")
        bPV, bX = bank("bPV"), bank("bX")
        bG, bGn = bank("bG"), bank("bGn")

        l_x = [sem(f"l_x{q}") for q in range(4)]
        l_w, l_mask, l_mask8 = sem("l_w"), sem("l_mask"), sem("l_mask8")
        l_gw, l_bias, l_h0 = sem("l_gw"), sem("l_bias"), sem("l_h0")
        l_rows, l_pieces = sem("l_rows"), sem("l_pieces")
        s_h0z, s_pool0, s_ident, s_identb, s_sel = sem("s_h0z"), sem("s_pool0"), sem("s_ident"), sem("s_identb"), sem("s_sel")
        s_fill, s_stkfill = sem("s_fill"), sem("s_stkfill")
        s_mrow, s_bhn, s_rows8 = sem("s_mrow"), sem("s_bhn"), sem("s_rows8")
        s_bhn_rows, s_bias_gi, s_half = sem("s_bhn_rows"), sem("s_bias_gi"), sem("s_half")
        s_wt, s_wT = sem("s_wt"), sem("s_wT")
        s_xp = sem("s_xp")
        s_proj, s_q1, s_rq, s_km, s_k1, s_rk, s_k2 = [sem(n) for n in (
            "s_proj", "s_q1", "s_rq", "s_km", "s_k1", "s_rk", "s_k2")]
        s_q2, s_q3, s_k3, s_v, s_xt = [sem(n) for n in ("s_q2", "s_q3", "s_k3", "s_v", "s_xt")]
        st1 = [sem(f"st1_{p}") for p in range(2)]
        st2 = [sem(f"st2_{p}") for p in range(2)]
        st_shift = [sem(f"st_shift{p}") for p in range(2)]
        s1_done, max_done, split_step, split_done = sem("s1_done"), sem("max_done"), sem("split_step"), sem("split_done")
        mxT_done, mxrow_done = sem("mxT_done"), sem("mxrow_done")
        s2_done, exp_done, vcur_done, pv_done = sem("s2_done"), sem("exp_done"), sem("vcur_done"), sem("pv_done")
        yT_done, yt_done, inv_done, norm_done = sem("yT_done"), sem("yt_done"), sem("inv_done"), sem("norm_done")
        x1_done, x1cur_done = sem("x1_done"), sem("x1cur_done")
        gimm_done, gib_done, gicur_done, sel_done = sem("gimm_done"), sem("gib_done"), sem("gicur_done"), sem("sel_done")
        rn_done, z_done = sem("rn_done"), sem("z_done")
        tr_done, tz_done, nt_done = sem("tr_done"), sem("tz_done"), sem("nt_done")
        hnT_done, trT_done, na_done, tzT_done = sem("hnT_done"), sem("trT_done"), sem("na_done"), sem("tzT_done")
        npre_done, zpart_done = sem("npre_done"), sem("zpart_done")
        h_ready, hh_done = sem("h_ready"), sem("hh_done")
        s_h0T, s_scan0, s_wihn = sem("s_h0T"), sem("s_scan0"), sem("s_wihn")
        gin_mm_done, gin_done = sem("gin_mm_done"), sem("gin_done")
        oT_done, outT_done, outev_done = sem("oT_done"), sem("outT_done"), sem("outev_done")
        st_out = [sem(f"st_out{p}") for p in range(2)]

        def slots(eng, slot):
            for it in range(-3, 1):
                for r in range(ITER):
                    slot(it, r)
            full = (H - LEAD_MAX - 1) // 2
            with eng.Fori(1, full) as it:
                for r in range(ITER):
                    slot(it, r)
            for it in range(full, STEPS // ITER):
                for r in range(ITER):
                    slot(it, r)
            for r in range(OCT):
                slot(STEPS // ITER, r)

        block = ctx.enter_context(nc.Block())

        @block.sync
        def _(sp):
            xv = x.rearrange("b c t -> c b t")
            x_v = x_sb[:, :].rearrange("c (b t) -> c b t", b=B)
            for q in range(4):
                sp.dma_start(x_v[:, 2 * q:2 * q + 2, :], xv[:, 2 * q:2 * q + 2, :]).then_inc(l_x[q], 16)
            for j in range(NJ):
                sp.dma_start(bias_n[32 * j:32 * j + 32, :],
                             b_ih.rearrange("(g j i f) -> g j f i", g=3, j=NJ, i=NI)[2, j],
                             allow_slow_non_contiguous=True).then_inc(l_bias, 16)
            sp.dma_start(mask_bc[:, :], mask.rearrange("b t -> (b t)").partition_broadcast(C)).then_inc(l_mask, 16)
            sp.wait_ge(s_h0z, 1)
            for j in range(NJ):
                sp.dma_start(h0[32 * j:32 * j + B, :], mask[:, W64 * j:W64 * (j + 1)]).then_inc(l_h0, 16)
            for w, dst in ((W_ih, wih), (W_hh, whh)):
                wv = w.rearrange("(j i f) n -> j f i n", j=NJ, i=NI)
                for j in range(NJ):
                    sp.dma_start(dst[32 * j:32 * j + 32, :, :], wv[j]).then_inc(l_gw, 16)
            sp.wait_ge(s_rows8, 1)
            sp.dma_start(row_dram.rearrange("r (b t) -> b r t", b=B), rows8[:, :, :]).then_inc(l_rows, 16)
            sp.wait_ge(l_rows, 16)
            sp.wait_ge(s_stkfill, 8)
            for par in range(2):
                sp.dma_start(stk1[par][1][0:3, :], row_dram[0:3]).then_inc(st1[par], 16)
                sp.dma_start(stk2[par][1][0:3, :], row_dram[0:3]).then_inc(st2[par], 16)
                sp.dma_start(stk2[par][1][ROW_M:NROW, :], row_dram[3:6]).then_inc(st2[par], 16)
            sp.wait_ge(l_pieces, 16 * 8)

            def load_stack(stk, at, h_):
                row = ROW_T
                for first, n in ((0, 3), (1, 2), (2, 1)):
                    qs = q_dram[first:first + 1, bass.ds(h_ * DH, DH), :]
                    for rep in range(n):
                        sp.dma_start(stk[0][row + rep * DH:row + (rep + 1) * DH, :], qs[0]).then_inc(at, 16)
                    ks = k_dram[0:n, bass.ds(h_ * DH, DH), :]
                    sp.dma_start(stk[1][row:row + n * DH, :], ks).then_inc(at, 16)
                    row += n * DH

            def slot(it, r):
                e, b = divmod(r, OCT)
                o = 2 * it + e
                if b == 0:
                    if live(o + LEAD_MAX + 1, H):
                        at_least(sp, s1_done, B * (o + LEAD_MAX))
                        par = (e + LEAD_MAX + 1) % 2
                        load_stack(stk1[par], st1[par], o + LEAD_MAX + 1)
                    if live(o + LEAD_EXP + 1, H):
                        at_least(sp, s2_done, B * (o + LEAD_EXP))
                        par = (e + LEAD_EXP + 1) % 2
                        load_stack(stk2[par], st2[par], o + LEAD_EXP + 1)
                if b == 4 and live(o + LEAD_ROW, H):
                    par = (e + LEAD_ROW) % 2
                    at_least(sp, mxrow_done, o + LEAD_ROW + 1)
                    for k in range(3):
                        sp.dma_start(stk2[par][0][ROW_M + k:ROW_M + k + 1, :].rearrange("p (a t) -> p a t", a=B * NI),
                                     mx_rows[B * NI * k:B * NI * (k + 1), :]).then_inc(st_shift[par], 16)
                if b == 0 and live(o - 2, H):
                    par = (e - 2) % 2
                    at_least(sp, outev_done, o - 1)
                    sp.dma_start(out[:, bass.ds((o - 2) * OCT, OCT), :].rearrange("b c t -> c b t"),
                                 o_sb[0:OCT * B, par, :]).then_inc(st_out[par], 16)

            slots(sp, slot)
            sp.wait_ge(outev_done, H)
            sp.dma_start(out[:, (H - 1) * OCT:, :].rearrange("b c t -> c b t"), o_sb[0:OCT * B, 1, :]).then_inc(st_out[1], 16)
            for par in range(2):
                sp.wait_ge(st_out[par], 16 * H // 2)

        @block.gpsimd
        def _(pool):
            pool.memset(ident[:, :], 0.0).then_inc(s_pool0, 1)
            pool.wait_ge(s_pool0, 1)
            pool.affine_select(out=ident[:, :], in_=ident[:, :], compare_op=ALU.not_equal, fill=1.0, base=0,
                               pattern=[[-1, 128]], channel_multiplier=1).then_inc(s_ident, 1)
            pool.wait_ge(s_ident, 1)
            pool.tensor_copy(identb[:, :], ident[:, :]).then_inc(s_identb, 1)
            pool.memset(sel[:, :, :], 0.0).then_inc(s_pool0, 1)
            pool.wait_ge(s_pool0, 2)
            pool.tensor_copy(sel[:, :, 0:B], ident[:, :].rearrange("p (s b) -> p s b", b=B)).then_inc(s_sel, 1)
            for t in (n_mul, n_add):
                pool.memset(t[:, :, :, :], 0.0).then_inc(s_scan0, 1)
            pool.memset(h_mul[:, :, :], 0.0).then_inc(s_scan0, 1)
            pool.memset(oT[:, :, :, :], 0.0).then_inc(s_scan0, 1)
            pool.memset(zero16[:, :], 0.0).then_inc(s_scan0, 1)
            pool.memset(half16[:, :], 0.5).then_inc(s_scan0, 1)
            pool.memset(mx_p[:, :, :], 0.0).then_inc(s_scan0, 1)
            pool.memset(v_cur[:, :, :], 0.0).then_inc(s_fill, 1)
            pool.memset(v_all[:, :, :, DH:EXT], 1.0).then_inc(s_fill, 1)
            pool.memset(ones_rows[:, :], 0.0).then_inc(s_fill, 1)
            pool.wait_ge(s_fill, 3)
            pool.memset(ones_rows[0:3, :], 1.0).then_inc(s_fill, 1)
            for n, stk in enumerate((*stk1, *stk2)):
                pool.memset(stk[1][0:ROW_T, :].bitcast(F32), 0.0).then_inc(s_stkfill, 1)
            for n, stk in enumerate((*stk1, *stk2)):
                pool.memset(stk[0][0:ROW_T, :].bitcast(F32), 0.0).then_inc(s_stkfill, 1)
                pool.wait_ge(s_stkfill, 5 + n)
                pool.memset(stk[0][0:3, :], 1.0).then_inc(s_fill, 1)
            for q in range(4):
                cs = slice(512 * q, 512 * (q + 1))
                pool.wait_ge(s_rq, q + 1)
                pool.tensor_copy(q_p[:, 1, cs], q_rest[:, cs]).then_inc(s_q2, 1)
                pool.wait_ge(s_q2, q + 1)
                pool.tensor_tensor(q_p[:, 2, cs], q_rest[:, cs], q_p[:, 1, cs], ALU.subtract).then_inc(s_q3, 1)
                pool.wait_ge(s_k2, q + 1)
                pool.tensor_tensor(k_p[:, 2, cs], k_rest[:, cs], k_p[:, 1, cs], ALU.subtract).then_inc(s_k3, 1)

            def zeros(*dims):
                return zero16[:, 0:1].rearrange("p (a b c) -> p a b c", a=1, b=1).to_broadcast([128, *dims])

            pool.wait_ge(l_gw, 128)
            for i in range(NI):
                pool.tensor_copy(wih_n[:, i, :, :].rearrange("p a (j f) -> p a j f", j=NJ),
                                 wih[:, i, 2 * T:3 * T].rearrange("p (j a f) -> p a j f", j=NJ, a=NI)).then_inc(s_wihn, 1)
            pool.wait_ge(s_scan0, 7)

            def slot(it, r):
                e, b = divmod(r, OCT)
                o, S = 2 * it + e, ITER * it + r
                if live(S, STEPS):
                    at_least(pool, h_ready, S + 1)
                    pool.tensor_tensor(hh[:, :], h_st[:, :, 1], half16[:, :], ALU.mult).then_inc(hh_done, 1)
                hm = o + LEAD_ROW
                if b == 0 and live(hm, H):
                    nm = neg_max[:, (e + LEAD_ROW) % 2, :]
                    at_least(pool, max_done, B * (hm + 1))
                    at_least(pool, mxT_done, hm)
                    pool.tensor_tensor(mx_p[:, 0, :], nm, zero16[:, :], ALU.add).then_inc(split_step, 1)
                    pool.wait_ge(split_step, 4 * hm + 1)
                    pool.tensor_tensor(mx_r[:, 0, :], nm, mx_p[:, 0, :], ALU.subtract).then_inc(split_step, 1)
                    pool.wait_ge(split_step, 4 * hm + 2)
                    pool.tensor_tensor(mx_p[:, 1, :], mx_r[:, 0, :], zero16[:, :], ALU.add).then_inc(split_step, 1)
                    pool.wait_ge(split_step, 4 * hm + 3)
                    pool.tensor_tensor(mx_r[:, 1, :], mx_r[:, 0, :], mx_p[:, 1, :], ALU.subtract).then_inc(split_step, 1)
                    pool.wait_ge(split_step, 4 * hm + 4)
                    pool.tensor_tensor(mx_p[:, 2, :], mx_r[:, 1, :], zero16[:, :], ALU.add).then_inc(split_done, 1)
                hv = o + LEAD_EXP
                if b == 1 and live(hv, H):
                    at_least(pool, pv_done, 2 * hv)
                    if isinstance(hv, int) and hv == 0:
                        pool.wait_ge(s_v, 4)
                        pool.wait_ge(s_fill, 4)
                    pool.tensor_tensor(v_cur[:, :, 0:EXT].unsqueeze(1), v_all[:, bass.ds(hv, 1), :, :], zeros(1, B * NI, EXT), ALU.add).then_inc(vcur_done, 1)
                for g, slot_add in ((0, 6), (1, 2)):
                    hy = o + LEAD_EXP - g
                    chans = bass.ds(hy * DH, DH)
                    rows = slice(GRP * g, GRP * g + GRP)
                    if b == slot_add and live(hy, H):
                        at_least(pool, norm_done, 2 * hy + g + 1)
                        if isinstance(hy, int) and hy == 0:
                            pool.wait_ge(s_xt, 4)
                        xv = xT[:, :, chans, rows].rearrange("p i c b -> p i b c")
                        pool.tensor_tensor(xv, y_n[:, :, :, :], xv, ALU.add).then_inc(x1_done, 1)
                        if g == 1:
                            add_current(it, e, g, hy)
                    if b == slot_add + 1 and g == 0 and live(hy, H):
                        add_current(it, e, g, hy)
                gp = it + 1
                if r == ITER - 1 and live(gp, STEPS // ITER):
                    at_least(pool, gib_done, 2 * gp + 2)
                    at_least(pool, sel_done, ITER * gp)
                    pool.tensor_tensor(gi_cur[:, 2:4, :], gi_next[:, 2:4, :],
                                       bias_gi[:, 2:4, :, :].rearrange("p j g c -> p j (g c)"), ALU.add).then_inc(gicur_done, 1)
                if live(S, STEPS):
                    if b == 0:
                        at_least(pool, outT_done, o - 1)
                        at_least(pool, x1_done, 2 * o + 2)
                    at_least(pool, h_ready, S + 2)
                    pool.tensor_tensor(oT[:, e, :, B * b:B * (b + 1)], h_st[:, :, 1].rearrange("p (i b) -> p i b", i=NI),
                                       xT[:, :, bass.ds(S, 1), :].rearrange("p i c b -> p i (c b)"), ALU.add).then_inc(oT_done, 1)

            def add_current(it, e, g, hy):
                chans = bass.ds(hy * DH, DH)
                rows = slice(GRP * g, GRP * g + GRP)
                at_least(pool, x1_done, 2 * hy + g + 1)
                par = (e + LEAD_EXP - g) % 2
                at_least(pool, gin_mm_done, it + (e + LEAD_EXP - g) // 2)
                pool.tensor_tensor(carrier[:, :], half16[:, 0:1], half16[:, 0:1], ALU.add)
                pool.tensor_tensor(x1_cur[:, :, par, :, rows], xT[:, :, chans, rows], zeros(NI, DH, GRP), ALU.add).then_inc(x1cur_done, 1)

            slots(pool, slot)

        @block.scalar
        def _(act):
            for n, w in enumerate((Wq, Wk, Wv)):
                act.dma_start(w_nat[:, n, :], w).then_inc(l_w, 16)
            act.dma_start(mask8[:, :], mask).then_inc(l_mask8, 16)
            act.dma_start(m8s[:, 0:1], att_b.partition_broadcast(B)).then_inc(l_mask8, 16)
            act.dma_start(bih_bc[:, :], b_ih.partition_broadcast(128)).then_inc(l_bias, 16)
            act.dma_start(bhh_bc[:, :], b_hh.partition_broadcast(128)).then_inc(l_bias, 16)
            act.wait_ge(s_wt, 1)
            nc.scalar.copy(wT[:, :, :], bX[:, 0:3 * C].rearrange("p (n o) -> p n o", n=3)).then_inc(s_wT, 1)
            for q in range(4):
                cs = slice(512 * q, 512 * (q + 1))
                act.wait_ge(s_proj, 4 * q + 1)
                nc.scalar.copy(q_p[:, 0, cs], bS1[:, :]).then_inc(s_q1, 1)
                act.wait_ge(s_km, q + 1)
                nc.scalar.copy(k_p[:, 0, cs], k_msk[:, cs]).then_inc(s_k1, 1)
                act.wait_ge(s_proj, 4 * q + 3)
                nc.scalar.copy(v_all[:, :, 4 * q:4 * q + 4, 0:DH],
                               bPV[:, :].rearrange("p (g h d) -> p h g d", g=4, h=H)).then_inc(s_v, 1)
                act.wait_ge(s_rk, q + 1)
                nc.scalar.copy(k_p[:, 1, cs], k_rest[:, cs]).then_inc(s_k2, 1)
                act.wait_ge(s_q3, q + 1)
                act.dma_start(q_dram[:, :, cs].rearrange("n c t -> c n t"), q_p[:, :, cs]).then_inc(l_pieces, 16)
                act.wait_ge(s_k3, q + 1)
                act.dma_start(k_dram[:, :, cs].rearrange("n c t -> c n t"), k_p[:, :, cs]).then_inc(l_pieces, 16)

            def slot(it, r):
                e, b = divmod(r, OCT)
                o, S = 2 * it + e, ITER * it + r
                gru = live(S, STEPS)
                if gru:
                    act.wait_ge(rn_done, S + 1)
                    nc.scalar.activation(tr[:, :], bN[:, 0:W64], ACT.Tanh, scale=0.5).then_inc(tr_done, 1)
                    act.wait_ge(z_done, S + 1)
                    nc.scalar.activation(tz[:, :], bZ[:, 0:W64], ACT.Tanh, scale=0.5).then_inc(tz_done, 1)
                for g, slot_ev in ((0, 5), (1, 1)):
                    hy = o + LEAD_EXP - g
                    if b == slot_ev and live(hy, H):
                        act.wait_ge(pv_done, 2 * hy + g + 1)
                        at_least(act, yt_done, 2 * hy + g)
                        nc.scalar.copy(yT[:, :], bPV[:, 0:T]).then_inc(yT_done, 1)
                hm = o + LEAD_ROW
                if b == 4 and live(hm, H):
                    act.wait_ge(mxT_done, hm + 1)
                    at_least(act, st_shift[(e + LEAD_ROW + 1) % 2], 48 * (it + (e + LEAD_ROW + 1) // 2))
                    nc.scalar.copy(mx_rows[:, :], bX[:, :].bitcast(BF16)[0:3 * B * NI, 0:128]).then_inc(mxrow_done, 1)
                if b == 0 and live(o - 2, H):
                    rows_out(o - 2, e, it - 1)
                gp = it + 1
                if r == ITER - 1 and live(gp, STEPS // ITER):
                    at_least(act, gib_done, 2 * gp + 1)
                    at_least(act, sel_done, ITER * gp)
                    nc.scalar.copy(gi_cur[:, 0:2, :], gi_next[:, 0:2, :]).then_inc(gicur_done, 1)
                if gru:
                    act.wait_ge(npre_done, S + 1)
                    nc.scalar.activation(h_mul[:, :, 1].rearrange("p (i b) -> p i b", i=NI), n_pre[:, :, 0:B, 1],
                                         ACT.Tanh).then_inc(nt_done, 1)
                if r == ITER - 1 and live(gp, STEPS // ITER):
                    act.wait_ge(gin_mm_done, gp + 1)
                    at_least(act, na_done, ITER * gp)
                    if isinstance(it, int) and it == -1:
                        act.wait_ge(l_bias, 16 * (2 + NJ))
                    for i in range(NI):
                        nc.scalar.activation(gin_cur[:, i, :, :].rearrange("p s b -> p (s b)"), bGn[:, 128 * i:128 * (i + 1)],
                                             ACT.Identity, bias=bias_n[:, i:i + 1]).then_inc(gin_done, 1)
                hp = o + LEAD_EXP
                if live(hp, H):
                    g, jj = divmod(b, GRP)
                    act.wait_ge(s2_done, B * hp + b + 1)
                    if jj == 0:
                        at_least(act, pv_done, 2 * (hp - 1) + g + 1)
                    nc.scalar.activation(probs[:, g, jj, :], bS2[:, :], ACT.Exp, scale=SCALE).then_inc(exp_done, 1)

            def rows_out(o, par, before):
                act.wait_ge(outT_done, o + 1)
                at_least(act, st_out[par], 16 * before)
                nc.scalar.copy(o_sb[:, par, :].rearrange("p (j i f) -> p i j f", j=NJ, i=NI),
                               bX[:, 0:T].rearrange("p (i j f) -> p i j f", i=NI, j=NJ)).then_inc(outev_done, 1)

            slots(act, slot)
            rows_out(H - 1, 1, H // 2 - 1)

        @block.vector
        def _(dve):
            dve.memset(h0[:, :], 0.0).then_inc(s_h0z, 1)
            dve.wait_ge(l_mask8, 32)
            chain = [0]

            def link(ins):
                chain[0] += 1
                ins.then_inc(s_mrow, 1)
                dve.wait_ge(s_mrow, chain[0])

            link(dve.tensor_scalar(m8[:, 0, :], mask8[:, :], 1.0, -NEG, ALU.subtract, ALU.mult))
            link(dve.tensor_reduce(m8s[:, 1:2], m8[:, 0, :], AX.X, ALU.max))
            link(dve.tensor_scalar(m8s[:, 2:3], m8s[:, 0:1], 1.0 / SCALE, None, ALU.mult))
            link(dve.tensor_scalar(m8[:, 1, :], m8[:, 0, :], m8s[:, 1:2], None, ALU.subtract))
            link(dve.scalar_tensor_tensor(out=m8[:, 2, :], in0=mask8[:, :], scalar=m8s[:, 2:3], in1=m8[:, 1, :],
                                          op0=ALU.mult, op1=ALU.add))

            def perm_out(ap):
                return ap.rearrange("p (i j f) -> p i j f", i=NI, j=NJ)

            def perm_in(ap):
                return ap.rearrange("p (j i f) -> p i j f", j=NJ, i=NI)

            link(dve.tensor_copy(perm_out(m8[:, 3, :]), perm_in(m8[:, 2, :])))
            link(dve.tensor_copy(rows8[:, 0, :], m8[:, 3, :]))
            link(dve.tensor_tensor(m8[:, 0, :], m8[:, 3, :], rows8[:, 0, :], ALU.subtract))
            link(dve.tensor_copy(rows8[:, 1, :], m8[:, 0, :]))
            link(dve.tensor_tensor(rows8[:, 2, :], m8[:, 0, :], rows8[:, 1, :], ALU.subtract))
            for k in range(3):
                last = dve.tensor_copy(perm_out(rows8[:, 3 + k, :]), perm_in(mask8[:, :]))
            last.then_inc(s_rows8, 1)

            for q in range(4):
                cs = slice(512 * q, 512 * (q + 1))
                dve.wait_ge(l_x[q], 16)
                for b in (2 * q, 2 * q + 1):
                    dve.tensor_copy(perm_out(xp[:, T * b:T * (b + 1)]), perm_in(x_sb[:, T * b:T * (b + 1)])).then_inc(s_xp, 1)
            dve.wait_ge(l_mask, 16)
            for q in range(4):
                cs = slice(512 * q, 512 * (q + 1))
                dve.wait_ge(s_proj, 4 * q + 2)
                for half in range(2):
                    b = 2 * q + half
                    mk = dve.tensor_tensor(perm_out(k_msk[:, T * b:T * (b + 1)]), perm_out(bS2[:, T * half:T * (half + 1)]),
                                           perm_in(mask_bc[:, T * b:T * (b + 1)]), ALU.mult)
                mk.then_inc(s_km, 1)
                dve.wait_ge(s_q1, q + 1)
                dve.tensor_tensor(q_rest[:, cs], bS1[:, :], q_p[:, 0, cs], ALU.subtract).then_inc(s_rq, 1)
                dve.wait_ge(s_k1, q + 1)
                dve.tensor_tensor(k_rest[:, cs], k_msk[:, cs], k_p[:, 0, cs], ALU.subtract).then_inc(s_rk, 1)
                dve.wait_ge(s_proj, 4 * q + 4)
                dve.tensor_copy(xT[:, :, :, 2 * q:2 * q + 2].rearrange("p i c b -> p b i c"),
                                bG[:, :].rearrange("p (b i c) -> p b i c", b=2, i=NI)).then_inc(s_xt, 1)

            def gru_setup():
                dve.wait_ge(l_gw, 16 * 8)
                dve.tensor_scalar(whh[:, :, 2 * T:3 * T], whh[:, :, 2 * T:3 * T], 0.5, None, ALU.mult).then_inc(s_half, 1)
                dve.wait_ge(l_bias, 16 * (2 + NJ))
                bi = bih_bc[:, :].rearrange("p (g j c) -> p g j c", g=3, j=NJ)
                bh = bhh_bc[:, :].rearrange("p (g j c) -> p g j c", g=3, j=NJ)
                bo = bias_gi[:, :, :, :].rearrange("p j g c -> p g j c")
                for g in range(2):
                    dve.tensor_tensor(bo[:, g], bi[:, g], bh[:, g], ALU.add).then_inc(s_bias_gi, 1)
                links = [0]

                def blink(ins):
                    links[0] += 1
                    ins.then_inc(s_bhn, 1)
                    dve.wait_ge(s_bhn, links[0])

                blink(dve.tensor_scalar(bhn_r[:, 0, :], bhh_bc[:, 2 * T:3 * T], 0.5, None, ALU.mult))
                blink(dve.tensor_copy(bhn_p[:, 0, :], bhn_r[:, 0, :]))
                blink(dve.tensor_tensor(bhn_r[:, 1, :], bhn_r[:, 0, :], bhn_p[:, 0, :], ALU.subtract))
                blink(dve.tensor_copy(bhn_p[:, 1, :], bhn_r[:, 1, :]))
                blink(dve.tensor_tensor(bhn_p[:, 2, :], bhn_r[:, 1, :], bhn_p[:, 1, :], ALU.subtract))
                dve.wait_ge(s_ident, 1)
                blink(dve.tensor_scalar(bhn_r[:, 0, :], bhn_p[:, 0, :], ident[:, 0:1], None, ALU.mult))
                blink(dve.scalar_tensor_tensor(out=bhn_r[:, 1, :], in0=bhn_p[:, 1, :], scalar=ident[:, 1:2],
                                               in1=bhn_r[:, 0, :], op0=ALU.mult, op1=ALU.add))
                dve.scalar_tensor_tensor(out=bhn_rows[:, :], in0=bhn_p[:, 2, :], scalar=ident[:, 2:3],
                                         in1=bhn_r[:, 1, :], op0=ALU.mult, op1=ALU.add).then_inc(s_bhn_rows, 1)
                dve.wait_ge(l_h0, 64)
                dve.wait_ge(s_h0z, 1)
                dve.transpose(h0T[:, :, :].rearrange("p i b -> p (i b)"), h0[:, :]).then_inc(s_h0T, 1)
                dve.wait_ge(s_h0T, 1)
                dve.tensor_copy(h_st[:, :, 1].rearrange("p (i b) -> p i b", i=NI), h0T[:, :, 0:B]).then_inc(h_ready, 1)
                dve.wait_ge(s_scan0, 7)

            def slot(it, r):
                e, b = divmod(r, OCT)
                o, S = 2 * it + e, ITER * it + r
                gru = live(S, STEPS)
                if isinstance(it, int) and it == -1 and r == OCT:
                    gru_setup()
                if gru:
                    dve.wait_ge(tr_done, S + 1)
                    dve.transpose(n_add[:, :, :, 0].rearrange("p i b -> p (i b)"), bN[:, W64:2 * W64]).then_inc(hnT_done, 1)
                    dve.transpose(n_mul[:, :, :, 1].rearrange("p i b -> p (i b)"), tr[:, :]).then_inc(trT_done, 1)
                    dve.wait_ge(hnT_done, S + 1)
                    if r == 0:
                        at_least(dve, gin_done, 2 * it + 2)
                    dve.tensor_tensor(n_add[:, :, 0:B, 1], n_add[:, :, 0:B, 0], gin_cur[:, :, r, :], ALU.add).then_inc(na_done, 1)
                    dve.wait_ge(tz_done, S + 1)
                    dve.transpose(tzT[:, :, :].rearrange("p i b -> p (i b)"), tz[:, :]).then_inc(tzT_done, 1)
                    dve.wait_ge(trT_done, S + 1)
                    dve.wait_ge(na_done, S + 1)
                    dve.tensor_tensor_scan(n_pre[:, :, :, :].rearrange("p i b e -> p (i b e)"),
                                           n_mul[:, :, :, :].rearrange("p i b e -> p (i b e)"),
                                           n_add[:, :, :, :].rearrange("p i b e -> p (i b e)"),
                                           0.0, ALU.mult, ALU.add).then_inc(npre_done, 1)
                    dve.wait_ge(tzT_done, S + 1)
                    dve.wait_ge(hh_done, S + 1)
                    dve.scalar_tensor_tensor(out=h_add[:, :, 1].rearrange("p (i b) -> p i b", i=NI), in0=tzT[:, :, 0:B], scalar=1.0,
                                             in1=hh[:, :].rearrange("p (i b) -> p i b", i=NI),
                                             op0=ALU.add, op1=ALU.mult).then_inc(zpart_done, 1)
                    dve.tensor_scalar(h_add[:, :, 0].rearrange("p (i b) -> p i b", i=NI), tzT[:, :, 0:B], -0.5, 0.5,
                                      ALU.mult, ALU.add).then_inc(zpart_done, 1)
                    dve.wait_ge(nt_done, S + 1)
                    dve.wait_ge(zpart_done, 2 * S + 2)
                    at_least(dve, oT_done, S)
                    dve.tensor_tensor_scan(h_st[:, :, :].rearrange("p a e -> p (a e)"), h_mul[:, :, :].rearrange("p a e -> p (a e)"),
                                           h_add[:, :, :].rearrange("p a e -> p (a e)"), 0.0, ALU.mult, ALU.add).then_inc(h_ready, 1)
                for g, slot_n in ((0, 6), (1, 2)):
                    hy = o + LEAD_EXP - g
                    if b == slot_n and live(hy, H):
                        yv = bX[:, 0:T].rearrange("p (i b d) -> p i b d", i=NI, b=GRP)
                        dve.wait_ge(yt_done, 2 * hy + g + 1)
                        at_least(dve, x1_done, 2 * hy + g)
                        dve.reciprocal(y_inv[:, :, :], yv[:, :, :, DH]).then_inc(inv_done, 1)
                        dve.wait_ge(inv_done, 2 * hy + g + 1)
                        dve.tensor_tensor(y_n[:, :, :, :], yv[:, :, :, 0:DH],
                                          y_inv[:, :, :].unsqueeze(3).to_broadcast([128, NI, GRP, DH]),
                                          ALU.mult).then_inc(norm_done, 1)
                gp = it + 1
                if r in (12, 13) and live(gp, STEPS // ITER):
                    half = r - 12
                    js = slice(2 * half, 2 * half + 2)
                    dve.wait_ge(gimm_done, 2 * gp + half + 1)
                    part = bG[:, 256 * half:256 * (half + 1)].rearrange("p (j c) -> p j c", j=2)
                    if half == 0:
                        at_least(dve, gicur_done, 2 * gp)
                        dve.tensor_tensor(gi_next[:, js, :], part, bias_gi[:, js, :, :].rearrange("p j g c -> p j (g c)"),
                                          ALU.add).then_inc(gib_done, 1)
                    else:
                        dve.tensor_copy(gi_next[:, js, :], part).then_inc(gib_done, 1)
                hx = o + LEAD_MAX
                if live(hx, H):
                    dve.wait_ge(s1_done, B * hx + b + 1)
                    if b == 0:
                        at_least(dve, split_done, hx - 1)
                    dve.tensor_reduce(neg_max[:, (e + LEAD_MAX) % 2, NI * b:NI * b + NI],
                                      bS1[:, :].rearrange("p (i k) -> p i k", i=NI), AX.X, ALU.max,
                                      negate=True).then_inc(max_done, 1)

            slots(dve, slot)

        @block.tensor
        def _(pe):
            pe.wait_ge(l_w, 48)
            pe.wait_ge(s_ident, 1)
            for n in range(3):
                last = nc.tensor.transpose(bX[:, C * n:C * (n + 1)], w_nat[:, n, :], ident[:, :])
            last.then_inc(s_wt, 1)
            pe.wait_ge(s_wT, 1)
            for q in range(4):
                cs = slice(512 * q, 512 * (q + 1))
                pe.wait_ge(s_xp, 2 * (q + 1))
                at_least(pe, s_rq, q)
                nc.tensor.matmul(bS1[:, :], wT[:, 0, :], xp[:, cs], start=True, stop=True).then_inc(s_proj, 1)
                at_least(pe, s_km, q)
                nc.tensor.matmul(bS2[:, :], wT[:, 1, :], xp[:, cs], start=True, stop=True).then_inc(s_proj, 1)
                at_least(pe, s_v, q)
                for g in range(4):
                    blk = xp[:, 512 * q + 128 * g:512 * q + 128 * (g + 1)]
                    last = nc.tensor.matmul(bPV[:, 128 * g:128 * (g + 1)], blk, wT[:, 2, :], start=True, stop=True)
                last.then_inc(s_proj, 1)
                at_least(pe, s_xt, q)
                for g in range(4):
                    blk = xp[:, 512 * q + 128 * g:512 * q + 128 * (g + 1)]
                    last = nc.tensor.transpose(bG[:, 128 * g:128 * (g + 1)], blk, ident[:, :])
                last.then_inc(s_proj, 1)
            pe.wait_ge(s_sel, 1)
            pe.wait_ge(s_identb, 1)
            pe.wait_ge(s_fill, 8)
            pe.wait_ge(s_rq, 4)
            pe.wait_ge(s_km, 4)
            pe.wait_ge(s_v, 4)
            pe.wait_ge(s_xt, 4)

            def hidden(bk, first, n):
                for i in range(NI):
                    for j in range(NJ):
                        w = whh[:, i, :].rearrange("p (g j c) -> p j g c", g=3, j=NJ)[:, j, first:first + 2 * n - 1:2]
                        last = nc.tensor.matmul(bk[32 * j:32 * j + B, 0:n * W64], h_st[:, B * i:B * (i + 1), 1], w,
                                                start=False, stop=(i == NI - 1), skip_group_check=True)
                return last

            def given(bk, s, g):
                for j in range(NJ):
                    last = nc.tensor.matmul(bk[32 * j:32 * j + 32, 0:W64], sel[:, s, :],
                                            gi_cur[:, j, W64 * g:W64 * (g + 1)],
                                            start=True, stop=False, skip_group_check=True)
                return last

            def slot(it, r):
                e, b = divmod(r, OCT)
                o, S = 2 * it + e, ITER * it + r
                if live(S, STEPS):
                    pe.wait_ge(h_ready, S + 1)
                    hidden(bN, 0, 2).then_inc(rn_done, 1)
                    hidden(bZ, 1, 1).then_inc(z_done, 1)
                ahead = live(S + 1, STEPS)
                s = (r + 1) % ITER
                if isinstance(it, int) and it == -1 and r == ITER - 1:
                    pe.wait_ge(s_bhn_rows, 1)
                    pe.wait_ge(s_half, 1)
                hx = o + LEAD_MAX
                if live(hx, H):
                    par = (e + LEAD_MAX) % 2
                    if b == 0:
                        pe.wait_ge(st1[par], 16 + 9 * 16 * (it + (e + LEAD_MAX) // 2 + 1))
                    at_least(pe, max_done, B * hx + b)
                    qs, ks = stk1[par]
                    for i in range(NI):
                        last = nc.tensor.matmul(bS1[:, T * i:T * (i + 1)], qs[0:ROW_M, T * b + 128 * i:T * b + 128 * (i + 1)],
                                                ks[0:ROW_M, T * b:T * (b + 1)], start=True, stop=True)
                    last.then_inc(s1_done, 1)
                if ahead and r < ITER - 1:
                    prepare(it, r, s, S)
                hp = o + LEAD_EXP
                if live(hp, H):
                    par = (e + LEAD_EXP) % 2
                    if b == 0:
                        n_th = it + (e + LEAD_EXP) // 2 + 1
                        pe.wait_ge(st2[par], 32 + 9 * 16 * n_th)
                        pe.wait_ge(st_shift[par], 48 * n_th)
                    at_least(pe, exp_done, B * hp + b)
                    qs, ks = stk2[par]
                    for i in range(NI):
                        last = nc.tensor.matmul(bS2[:, T * i:T * (i + 1)], ks[0:NROW, T * b + 128 * i:T * b + 128 * (i + 1)],
                                                qs[0:NROW, T * b:T * (b + 1)], start=True, stop=True)
                    last.then_inc(s2_done, 1)
                for g, slot_pv in ((0, 4), (1, 0)):
                    hy = o + LEAD_EXP - g
                    if b == slot_pv and live(hy, H):
                        pe.wait_ge(exp_done, B * hy + GRP * (g + 1))
                        pe.wait_ge(vcur_done, hy + 1)
                        at_least(pe, yT_done, 2 * hy + g)
                        for i in range(NI):
                            for jj in range(GRP):
                                last = nc.tensor.matmul(bPV[32 * jj:32 * jj + 32, 0:T], v_cur[:, NI * (GRP * g + jj) + i, :],
                                                        probs[:, g, jj, T * i:T * (i + 1)],
                                                        start=(i == 0), stop=(i == NI - 1), skip_group_check=True)
                        last.then_inc(pv_done, 1)
                    if b == slot_pv + 1 and live(hy, H):
                        pe.wait_ge(yT_done, 2 * hy + g + 1)
                        if g == 0:
                            at_least(pe, mxrow_done, o + LEAD_ROW + 1, H)
                        else:
                            at_least(pe, outev_done, o - 1)
                            at_least(pe, norm_done, 2 * hy + 1)
                        for i in range(NI):
                            last = nc.tensor.transpose(bX[:, 128 * i:128 * (i + 1)], yT[:, 128 * i:128 * (i + 1)], ident[:, :])
                        last.then_inc(yt_done, 1)
                hm = o + LEAD_ROW
                if b == 3 and live(hm, H):
                    pe.wait_ge(split_done, hm + 1)
                    at_least(pe, norm_done, 2 * (o + LEAD_EXP))
                    nc.tensor.transpose(bX[:, :].bitcast(BF16)[:, 0:128],
                                        mx_p[:, :, :].rearrange("p n a -> p (n a)"), identb[:, :]).then_inc(mxT_done, 1)
                gp = it + 1
                if r in (11, 12) and live(gp, STEPS // ITER):
                    half = r - 11
                    at_least(pe, x1cur_done, 4 * (gp + 1))
                    if isinstance(it, int) and it == -1:
                        pe.wait_ge(l_gw, 128)
                    at_least(pe, gib_done, 2 * gp + half)
                    for j in range(2 * half, 2 * half + 2):
                        for i in range(NI):
                            last = nc.tensor.matmul(bG[:, 128 * j:128 * (j + 1)], x1_cur[:, i, :, :, :].rearrange("p a c b -> p (a c b)"),
                                                    wih[:, i, :].rearrange("p (g j c) -> p j g c", g=3, j=NJ)[:, j, 0:2],
                                                    start=(i == 0), stop=(i == NI - 1))
                    last.then_inc(gimm_done, 1)
                if r == 13 and live(gp, STEPS // ITER):
                    at_least(pe, gin_done, NI * gp)
                    if isinstance(it, int) and it == -1:
                        pe.wait_ge(s_wihn, NI)
                    for io in range(NI):
                        for i in range(NI):
                            last = nc.tensor.matmul(bGn[:, 128 * io:128 * (io + 1)], wih_n[:, i, io, :],
                                                    x1_cur[:, i, :, :, :].rearrange("p a c b -> p (a c b)"),
                                                    start=(i == 0), stop=(i == NI - 1))
                    last.then_inc(gin_mm_done, 1)
                if b == OCT - 1 and live(o - 1, H):
                    transpose_out(o - 1, (e + 1) % 2)
                if ahead and r == ITER - 1:
                    prepare(it, r, s, S)

            def prepare(it, r, s, S):
                if r == ITER - 1:
                    pe.wait_ge(gicur_done, 2 * (it + 1) + 2)
                at_least(pe, hnT_done, S + 1)
                given(bN, s, 0)
                for j in range(NJ):
                    nc.tensor.matmul(bN[32 * j:32 * j + 32, W64:2 * W64], ones_rows[:, :], bhn_rows[:, W64 * j:W64 * (j + 1)],
                                     start=False, stop=False, skip_group_check=True)
                at_least(pe, tz_done, S + 1)
                given(bZ, s, 1).then_inc(sel_done, 1)

            def transpose_out(o, par):
                pe.wait_ge(oT_done, OCT * (o + 1))
                at_least(pe, outev_done, o)
                at_least(pe, norm_done, 2 * (o + 1 + LEAD_EXP) + 1, 2 * H)
                for i in range(NI):
                    last = nc.tensor.transpose(bX[:, 128 * i:128 * (i + 1)], oT[:, par, i, :], ident[:, :])
                last.then_inc(outT_done, 1)

            slots(pe, slot)


_INS = ['x', 'cond_2048', 'L0_cond_Wq', 'L0_cond_Wk', 'L0_cond_Wv', 'L0_cond_b',
        'L1_cond_W_ih', 'L1_cond_W_hh', 'L1_cond_b_ih', 'L1_cond_b_hh']


def kernel(**inputs):
    import numpy as np
    import concourse.bacc as bacc
    from concourse.bass_utils import run_bass_kernel_spmd

    nc = bacc.Bacc("TRN2", target_bir_lowering=False, num_devices=1)
    arrays, args = {}, []
    for name in _INS:
        a = np.ascontiguousarray(inputs[name])
        arrays[f"in_{name}"] = a
        args.append(nc.dram_tensor(f"in_{name}", a.shape, mybir.dt.from_np(a.dtype), kind="ExternalInput").ap())
    out = nc.dram_tensor("out_x", [B, C, T], F32, kind="ExternalOutput").ap()
    build(nc, *args, out)
    r = run_bass_kernel_spmd(nc, [arrays], core_ids=[0])
    return r.results[0]["out_x"]
```

```python
from contextlib import ExitStack

import concourse.bass as bass
from concourse import mybir

F32 = mybir.dt.float32
BF16 = mybir.dt.bfloat16
ACT = mybir.ActivationFunctionType
ALU = mybir.AluOpType
AX = mybir.AxisListType

B = 8
C = 128
T = 256
H = 16
DH = C // H
NI = T // 128
NJ = 4
W64 = T // NJ
BT = B * T
OCT = 8
ITER = 2 * OCT
STEPS = C
GRP = 4
EXT = DH + 1
LEAD_MAX, LEAD_ROW, LEAD_EXP = 5, 4, 3
TERMS = 9 * DH
ROW_T = 32
ROW_M = ROW_T + TERMS
NROW = ROW_M + 3
SCALE = float(DH) ** -0.5
NEG = -1e30 / SCALE


def live(n, end):
    return not isinstance(n, int) or 0 <= n < end


def at_least(eng, sem, n, most=1 << 20):
    if isinstance(n, int):
        if n <= 0:
            return
        n = min(n, most)
    eng.wait_ge(sem, n)


def build(nc, x, mask, Wq, Wk, Wv, att_b, W_ih, W_hh, b_ih, b_hh, out):
    with ExitStack() as ctx:
        def sb(name, shape, dt=F32):
            return ctx.enter_context(nc.sbuf_tensor(name, shape, dt))

        def bank(name):
            return ctx.enter_context(nc.psum_tensor(name, [128, 512], F32))

        def sem(name):
            return ctx.enter_context(nc.semaphore(name))

        q_dram = nc.dram_tensor("q_pieces", [H, 3, DH, BT], BF16).ap()
        k_dram = nc.dram_tensor("k_pieces", [H, DH, 3, BT], BF16).ap()
        row_dram = nc.dram_tensor("mask_rows", [6, BT], BF16).ap()

        x_sb = sb("x_sb", [C, BT])
        xp = sb("xp", [C, BT])
        mask_bc = sb("mask_bc", [C, BT])
        w_nat = sb("w_nat", [C, 3, C])
        wT = sb("wT", [C, 3, C])
        wih = sb("wih", [128, NI, 3 * T])
        wih_n = sb("wih_n", [128, NI, NI, 128])
        whh = sb("whh", [128, NI, 3 * T])
        bih_bc = sb("bih_bc", [128, 3 * T])
        bhh_bc = sb("bhh_bc", [128, 3 * T])
        bias_gi = sb("bias_gi", [128, NJ, 2, W64])
        bias_n = sb("bias_n", [128, NI])
        bhn_p = sb("bhn_p", [128, 3, T], BF16)
        bhn_r = sb("bhn_r", [128, 2, T])
        bhn_rows = sb("bhn_rows", [128, T], BF16)
        ones_rows = sb("ones_rows", [128, 32], BF16)
        ident = sb("ident", [128, 128])
        identb = sb("identb", [128, 128], BF16)
        sel = sb("sel", [128, ITER, 32])
        mask8 = sb("mask8", [B, T])
        m8 = sb("m8", [B, 4, T])
        m8s = sb("m8s", [B, 4])
        rows8 = sb("rows8", [B, 6, T], BF16)
        q_p = sb("q_p", [C, 3, BT], BF16)
        k_p = sb("k_p", [C, 3, BT], BF16)
        q_rest = sb("q_rest", [C, BT])
        k_msk = sb("k_msk", [C, BT])
        k_rest = sb("k_rest", [C, BT])
        v_all = sb("v_all", [128, H, B * NI, EXT])
        xT = sb("xT", [128, NI, C, B])

        q_stk = sb("q_stk", [128, 4, BT], BF16)
        k_stk = sb("k_stk", [128, 4, BT], BF16)
        stk1 = [[t[:, par, :] for t in (q_stk, k_stk)] for par in range(2)]
        stk2 = [[t[:, 2 + par, :] for t in (q_stk, k_stk)] for par in range(2)]
        neg_max = sb("neg_max", [128, 2, B * NI])
        mx_p = sb("mx_p", [128, 8, B * NI], BF16)
        mx_r = sb("mx_r", [128, 2, B * NI])
        zero16 = sb("zero16", [128, NI * B])
        half16 = sb("half16", [128, NI * B])
        warm = sb("warm", [128, 1])
        carrier = sb("carrier", [128, 1])
        mx_rows = sb("mx_rows", [3 * B * NI, 128], BF16)
        v_cur = sb("v_cur", [128, B * NI, 32])
        probs = sb("probs", [128, 2, GRP, NI * T])
        yT = sb("yT", [128, T])
        y_inv = sb("y_inv", [128, NI, GRP])
        y_n = sb("y_n", [128, NI, GRP, DH])
        x1_cur = sb("x1_cur", [128, NI, 2, DH, B])
        gi_next = sb("gi_next", [128, NJ, 2 * W64])
        gi_cur = sb("gi_cur", [128, NJ, 2 * W64])
        gin_cur = sb("gin_cur", [128, NI, ITER, B])

        h0 = sb("h0", [128, W64])
        h0T = sb("h0T", [128, NI, 32])
        tr = sb("tr", [128, W64])
        tz = sb("tz", [128, W64])
        tzT = sb("tzT", [128, NI, 32])
        hh = sb("hh", [128, NI * B])
        rn = sb("rn", [128, W64])
        rnT = sb("rnT", [128, NI, 32])
        n_pre = sb("n_pre", [128, NI, B])
        h_mul = sb("h_mul", [128, NI * B, 2])
        h_add = sb("h_add", [128, NI * B, 2])
        h_st = sb("h_st", [128, NI * B, 2])
        oT = sb("oT", [128, 2, NI, 128])
        o_sb = sb("o_sb", [128, 2, T])

        bN, bZ = bank("bN"), bank("bZ")
        bS1, bS2 = bank("bS1"), bank("bS2")
        bPV, bX = bank("bPV"), bank("bX")
        bG, bGn = bank("bG"), bank("bGn")

        l_x = [sem(f"l_x{q}") for q in range(4)]
        l_w, l_mask, l_mask8 = sem("l_w"), sem("l_mask"), sem("l_mask8")
        l_gw, l_bias, l_h0 = sem("l_gw"), sem("l_bias"), sem("l_h0")
        l_rows, l_pieces = sem("l_rows"), sem("l_pieces")
        s_h0z, s_pool0, s_ident, s_identb, s_sel = sem("s_h0z"), sem("s_pool0"), sem("s_ident"), sem("s_identb"), sem("s_sel")
        s_fill, s_stkfill, s_kfill, s_warm = sem("s_fill"), sem("s_stkfill"), sem("s_kfill"), sem("s_warm")
        s_mrow, s_bhn, s_rows8 = sem("s_mrow"), sem("s_bhn"), sem("s_rows8")
        s_bhn_rows, s_bias_gi, s_half = sem("s_bhn_rows"), sem("s_bias_gi"), sem("s_half")
        s_wt, s_wT = sem("s_wt"), sem("s_wT")
        s_xp = sem("s_xp")
        s_proj, s_q1, s_rq, s_km, s_k1, s_rk, s_k2 = [sem(n) for n in (
            "s_proj", "s_q1", "s_rq", "s_km", "s_k1", "s_rk", "s_k2")]
        s_q2, s_q3, s_k3, s_last3, s_extra, s_v, s_xt = [sem(n) for n in ("s_q2", "s_q3", "s_k3", "s_last3", "s_extra", "s_v", "s_xt")]
        st1 = [sem(f"st1_{p}") for p in range(2)]
        st_first, st_mask = sem("st_first"), sem("st_mask")
        st2 = [sem(f"st2_{p}") for p in range(2)]
        st_shift = [sem(f"st_shift{p}") for p in range(2)]
        s1_done, max_done, split_step, split_done = sem("s1_done"), sem("max_done"), sem("split_step"), sem("split_done")
        mxT_done, mxrow_done = sem("mxT_done"), sem("mxrow_done")
        s2_done, exp_done, vcur_done, pv_done = sem("s2_done"), sem("exp_done"), sem("vcur_done"), sem("pv_done")
        yT_done, yt_done, inv_done, norm_done = sem("yT_done"), sem("yt_done"), sem("inv_done"), sem("norm_done")
        x1_done, x1cur_done = sem("x1_done"), sem("x1cur_done")
        gimm_done, gib_done, gicur_done, sel_done = sem("gimm_done"), sem("gib_done"), sem("gicur_done"), sem("sel_done")
        rn_done, z_done = sem("rn_done"), sem("z_done")
        tr_done, tz_done, nt_done = sem("tr_done"), sem("tz_done"), sem("nt_done")
        rn_used, rnT_done, tzT_done = sem("rn_used"), sem("rnT_done"), sem("tzT_done")
        npre_done, zh_done, omz_done = sem("npre_done"), sem("zh_done"), sem("omz_done")
        h_ready, hh_done = sem("h_ready"), sem("hh_done")
        s_h0T, s_scan0, s_wihn = sem("s_h0T"), sem("s_scan0"), sem("s_wihn")
        gin_mm_done, gin_done = sem("gin_mm_done"), sem("gin_done")
        oT_done, outT_done, outev_done = sem("oT_done"), sem("outT_done"), sem("outev_done")
        st_out = [sem(f"st_out{p}") for p in range(2)]

        def extra_bank(o, q):
            return (bPV, bG, bGn)[(q + o + 5) % 3]

        def rows_slot(o):
            return 2 if isinstance(o, int) and o < -2 else 3

        def score_bank(S, odd, bk, other):
            return other if isinstance(S, int) and S < -2 and odd else bk

        def free_below(S, n):
            return n - 1 if isinstance(S, int) and S < -2 else n

        def slots(eng, slot):
            for it in range(-3, 1):
                for r in range(ITER):
                    slot(it, r)
            full = (H - LEAD_MAX - 1) // 2
            with eng.Fori(1, full) as it:
                for r in range(ITER):
                    slot(it, r)
            for it in range(full, STEPS // ITER):
                for r in range(ITER):
                    slot(it, r)
            for r in range(OCT):
                slot(STEPS // ITER, r)

        block = ctx.enter_context(nc.Block())

        @block.sync
        def _(sp):
            xv = x.rearrange("b c t -> c b t")
            x_v = x_sb[:, :].rearrange("c (b t) -> c b t", b=B)
            for q in range(4):
                sp.dma_start(x_v[:, 2 * q:2 * q + 2, :], xv[:, 2 * q:2 * q + 2, :]).then_inc(l_x[q], 16)
            for j in range(NJ):
                sp.dma_start(bias_n[32 * j:32 * j + 32, :],
                             b_ih.rearrange("(g j i f) -> g j f i", g=3, j=NJ, i=NI)[2, j],
                             allow_slow_non_contiguous=True).then_inc(l_bias, 16)
            sp.dma_start(mask_bc[:, :], mask.rearrange("b t -> (b t)").partition_broadcast(C)).then_inc(l_mask, 16)
            sp.wait_ge(s_h0z, 1)
            sp.wait_ge(s_warm, 1)
            for j in range(NJ):
                sp.dma_start(h0[32 * j:32 * j + B, :], mask[:, W64 * j:W64 * (j + 1)]).then_inc(l_h0, 16)
            for w, dst in ((W_ih, wih), (W_hh, whh)):
                wv = w.rearrange("(j i f) n -> j f i n", j=NJ, i=NI)
                for j in range(NJ):
                    sp.dma_start(dst[32 * j:32 * j + 32, :, :], wv[j]).then_inc(l_gw, 16)
            sp.wait_ge(s_rows8, 1)
            sp.dma_start(row_dram.rearrange("r (b t) -> b r t", b=B), rows8[:, :, :]).then_inc(l_rows, 16)
            sp.wait_ge(l_rows, 16)
            sp.wait_ge(s_kfill, 1)
            sp.dma_start(k_stk[0:3, :, :], row_dram[0:3].unsqueeze(1).to_broadcast([3, 4, BT])).then_inc(st_mask, 16)
            sp.dma_start(k_stk[ROW_M:NROW, 2:4, :], row_dram[3:6].unsqueeze(1).to_broadcast([3, 2, BT])).then_inc(st_mask, 16)

            def load_stack(stk, at, h_):
                sp.dma_start(stk[0][ROW_T:ROW_M, :], q_dram[bass.ds(h_, 1)].rearrange("h p d t -> (h p d) t").unsqueeze(1).to_broadcast([3 * DH, 3, BT])).then_inc(at, 16)
                sp.dma_start(stk[1][ROW_T:ROW_M, :], k_dram[bass.ds(h_, 1)].rearrange("h d p t -> h (d p) t").to_broadcast([3, 3 * DH, BT])).then_inc(at, 16)

            for half, at in ((0, st_first), (1, st1[0])):
                sp.wait_ge(s_k3, 2 + half)
                if half == 1:
                    sp.wait_ge(s_last3, 2)
                cs = slice(BT // 2 * half, BT // 2 * (half + 1))
                for p in range(3):
                    rows = slice(ROW_T + 3 * DH * p, ROW_T + 3 * DH * (p + 1))
                    sp.dma_start(stk1[0][0][rows, cs], q_p[0:DH, p:p + 1, cs].to_broadcast([DH, 3, BT // 2])).then_inc(at, 16)
                    sp.dma_start(stk1[0][1][rows, cs], k_p[0:DH, :, cs]).then_inc(at, 16)
            sp.wait_ge(l_pieces, 80)
            load_stack(stk1[1], st1[1], 1)
            for h_ in range(2):
                load_stack(stk2[h_], st2[h_], h_)

            def slot(it, r):
                e, b = divmod(r, OCT)
                o = 2 * it + e
                if b == 0:
                    if live(o + LEAD_MAX - 1, H - 2):
                        at_least(sp, s1_done, B * (o + LEAD_MAX))
                        par = (e + LEAD_MAX + 1) % 2
                        load_stack(stk1[par], st1[par], o + LEAD_MAX + 1)
                    if live(o + LEAD_EXP - 1, H - 2):
                        at_least(sp, s2_done, B * (o + LEAD_EXP))
                        par = (e + LEAD_EXP + 1) % 2
                        load_stack(stk2[par], st2[par], o + LEAD_EXP + 1)
                if b == rows_slot(o) + 1 and live(o + LEAD_ROW, H):
                    par = (e + LEAD_ROW) % 2
                    at_least(sp, mxrow_done, o + LEAD_ROW + 1)
                    sp.dma_start(stk2[par][0][ROW_M:NROW, :].rearrange("p (a t) -> p a t", a=B * NI),
                                 mx_rows[:, :]).then_inc(st_shift[par], 16)
                if b == 0 and live(o - 2, H):
                    par = (e - 2) % 2
                    at_least(sp, outev_done, o - 1)
                    sp.dma_start(out[:, bass.ds((o - 2) * OCT, OCT), :].rearrange("b c t -> c b t"),
                                 o_sb[0:OCT * B, par, :]).then_inc(st_out[par], 16)

            slots(sp, slot)
            sp.wait_ge(outev_done, H)
            sp.dma_start(out[:, (H - 1) * OCT:, :].rearrange("b c t -> c b t"), o_sb[0:OCT * B, 1, :]).then_inc(st_out[1], 16)
            for par in range(2):
                sp.wait_ge(st_out[par], 16 * H // 2)

        @block.gpsimd
        def _(pool):
            pool.memset(ident[:, :], 0.0).then_inc(s_pool0, 1)
            pool.wait_ge(s_pool0, 1)
            pool.affine_select(out=ident[:, :], in_=ident[:, :], compare_op=ALU.not_equal, fill=1.0, base=0,
                               pattern=[[-1, 128]], channel_multiplier=1).then_inc(s_ident, 1)
            pool.wait_ge(s_ident, 1)
            pool.tensor_copy(identb[:, :], ident[:, :]).then_inc(s_identb, 1)
            pool.memset(sel[:, :, :], 0.0).then_inc(s_pool0, 1)
            pool.wait_ge(s_pool0, 2)
            pool.tensor_copy(sel[:, :, 0:B], ident[:, :].rearrange("p (s b) -> p s b", b=B)).then_inc(s_sel, 1)
            pool.memset(h_mul[:, :, :], 0.0).then_inc(s_scan0, 1)
            pool.memset(oT[:, :, :, :], 0.0).then_inc(s_scan0, 1)
            pool.memset(zero16[:, :], 0.0).then_inc(s_scan0, 1)
            pool.memset(half16[:, :], 0.5).then_inc(s_scan0, 1)
            pool.memset(mx_p[:, :, :], 0.0).then_inc(s_scan0, 1)
            pool.memset(v_cur[:, :, :], 0.0).then_inc(s_fill, 1)
            pool.memset(v_all[:, :, :, DH:EXT], 1.0).then_inc(s_fill, 1)
            pool.memset(ones_rows[:, :], 0.0).then_inc(s_fill, 1)
            pool.wait_ge(s_fill, 3)
            pool.memset(ones_rows[0:3, :], 1.0).then_inc(s_fill, 1)
            pool.memset(q_stk[0:ROW_T, :, :].bitcast(F32), 0.0).then_inc(s_stkfill, 1)
            pool.wait_ge(s_stkfill, 1)
            pool.memset(q_stk[0:3, :, :], 1.0).then_inc(s_fill, 1)
            for q in range(3):
                cs = slice(512 * q, 512 * (q + 1))
                pool.wait_ge(s_q2, q + 1)
                pool.tensor_tensor(q_p[:, 2, cs], q_rest[:, cs], q_p[:, 1, cs], ALU.subtract).then_inc(s_q3, 1)
                pool.wait_ge(s_k2, q + 1)
                pool.tensor_tensor(k_p[:, 2, cs], k_rest[:, cs], k_p[:, 1, cs], ALU.subtract).then_inc(s_k3, 1)

            def zeros(*dims):
                return zero16[:, 0:1].rearrange("p (a b c) -> p a b c", a=1, b=1).to_broadcast([128, *dims])

            pool.wait_ge(l_gw, 128)
            for i in range(NI):
                pool.tensor_copy(wih_n[:, i, :, :].rearrange("p a (j f) -> p a j f", j=NJ),
                                 wih[:, i, 2 * T:3 * T].rearrange("p (j a f) -> p a j f", j=NJ, a=NI)).then_inc(s_wihn, 1)
            pool.wait_ge(s_scan0, 5)

            def slot(it, r):
                e, b = divmod(r, OCT)
                o, S = 2 * it + e, ITER * it + r
                if live(S, STEPS):
                    at_least(pool, h_ready, S + 1)
                    pool.tensor_tensor(hh[:, :], h_st[:, :, 1], half16[:, :], ALU.mult).then_inc(hh_done, 1)
                hm = o + LEAD_ROW
                if b == 0 and live(hm, H):
                    nm = neg_max[:, (e + LEAD_ROW) % 2, :]
                    at_least(pool, max_done, B * (hm + 1))
                    at_least(pool, mxT_done, hm)
                    pool.tensor_tensor(mx_p[:, 0, :], nm, zero16[:, :], ALU.add).then_inc(split_step, 1)
                    pool.wait_ge(split_step, 4 * hm + 1)
                    pool.tensor_tensor(mx_r[:, 0, :], nm, mx_p[:, 0, :], ALU.subtract).then_inc(split_step, 1)
                    pool.wait_ge(split_step, 4 * hm + 2)
                    pool.tensor_tensor(mx_p[:, 1, :], mx_r[:, 0, :], zero16[:, :], ALU.add).then_inc(split_step, 1)
                    pool.wait_ge(split_step, 4 * hm + 3)
                    pool.tensor_tensor(mx_r[:, 1, :], mx_r[:, 0, :], mx_p[:, 1, :], ALU.subtract).then_inc(split_step, 1)
                    pool.wait_ge(split_step, 4 * hm + 4)
                    pool.tensor_tensor(mx_p[:, 2, :], mx_r[:, 1, :], zero16[:, :], ALU.add).then_inc(split_done, 1)
                hv = o + LEAD_EXP
                if b == 1 and live(hv, H):
                    at_least(pool, pv_done, 2 * hv)
                    if isinstance(hv, int) and hv == 0:
                        pool.wait_ge(s_v, 4)
                        pool.wait_ge(s_fill, 4)
                    pool.tensor_tensor(v_cur[:, :, 0:EXT].unsqueeze(1), v_all[:, bass.ds(hv, 1), :, :], zeros(1, B * NI, EXT), ALU.add).then_inc(vcur_done, 1)
                for g, slot_add in ((0, 6), (1, 2)):
                    hy = o + LEAD_EXP - g
                    chans = bass.ds(hy * DH, DH)
                    rows = slice(GRP * g, GRP * g + GRP)
                    if b == slot_add and live(hy, H):
                        at_least(pool, norm_done, 2 * hy + g + 1)
                        if isinstance(hy, int) and hy == 0:
                            pool.wait_ge(s_xt, 4)
                        xv = xT[:, :, chans, rows].rearrange("p i c b -> p i b c")
                        pool.tensor_tensor(xv, y_n[:, :, :, :], xv, ALU.add).then_inc(x1_done, 1)
                        if g == 1:
                            add_current(it, e, g, hy)
                    if b == slot_add + 1 and g == 0 and live(hy, H):
                        add_current(it, e, g, hy)
                gp = it + 1
                if r == ITER - 1 and live(gp, STEPS // ITER):
                    at_least(pool, gib_done, 2 * gp + 2)
                    at_least(pool, sel_done, ITER * gp)
                    pool.tensor_tensor(gi_cur[:, 2:4, :], gi_next[:, 2:4, :],
                                       bias_gi[:, 2:4, :, :].rearrange("p j g c -> p j (g c)"), ALU.add).then_inc(gicur_done, 1)
                if live(S, STEPS):
                    if b == 0:
                        at_least(pool, outT_done, o - 1)
                        at_least(pool, x1_done, 2 * o + 2)
                    at_least(pool, h_ready, S + 2)
                    pool.tensor_tensor(oT[:, e, :, B * b:B * (b + 1)], h_st[:, :, 1].rearrange("p (i b) -> p i b", i=NI),
                                       xT[:, :, bass.ds(S, 1), :].rearrange("p i c b -> p i (c b)"), ALU.add).then_inc(oT_done, 1)

            def add_current(it, e, g, hy):
                chans = bass.ds(hy * DH, DH)
                rows = slice(GRP * g, GRP * g + GRP)
                at_least(pool, x1_done, 2 * hy + g + 1)
                par = (e + LEAD_EXP - g) % 2
                at_least(pool, gin_mm_done, it + (e + LEAD_EXP - g) // 2)
                pool.tensor_tensor(carrier[:, :], half16[:, 0:1], half16[:, 0:1], ALU.add)
                pool.tensor_tensor(x1_cur[:, :, par, :, rows], xT[:, :, chans, rows], zeros(NI, DH, GRP), ALU.add).then_inc(x1cur_done, 1)

            slots(pool, slot)

        @block.scalar
        def _(act):
            for n, w in enumerate((Wq, Wk, Wv)):
                act.dma_start(w_nat[:, n, :], w).then_inc(l_w, 16)
            act.wait_ge(s_h0z, 1)
            nc.scalar.activation(warm[:, :], h0[:, 0:1], ACT.Exp).then_inc(s_warm, 1)
            act.dma_start(mask8[:, :], mask).then_inc(l_mask8, 16)
            act.dma_start(m8s[:, 0:1], att_b.partition_broadcast(B)).then_inc(l_mask8, 16)
            act.dma_start(bih_bc[:, :], b_ih.partition_broadcast(128)).then_inc(l_bias, 16)
            act.dma_start(bhh_bc[:, :], b_hh.partition_broadcast(128)).then_inc(l_bias, 16)
            act.wait_ge(s_wt, 1)
            nc.scalar.copy(wT[:, :, :], bX[:, 0:3 * C].rearrange("p (n o) -> p n o", n=3)).then_inc(s_wT, 1)
            for b in range(B):
                act.wait_ge(l_x[b // 2], 16)
                nc.scalar.copy(xp[:, T * b:T * (b + 1)].rearrange("p (i j f) -> p i j f", i=NI, j=NJ),
                               x_sb[:, T * b:T * (b + 1)].rearrange("p (j i f) -> p i j f", j=NJ, i=NI)).then_inc(s_xp, 1)
            for q in range(5):
                if q < 4:
                    cs = slice(512 * q, 512 * (q + 1))
                    act.wait_ge(s_proj, 2 * q + 1)
                    nc.scalar.copy(q_p[:, 0, cs], (bS1, bN)[q % 2][:, :]).then_inc(s_q1, 1)
                    act.wait_ge(s_km, q + 1)
                    nc.scalar.copy(k_p[:, 0, cs], k_msk[:, cs]).then_inc(s_k1, 1)
                if q > 0:
                    cs = slice(512 * (q - 1), 512 * q)
                    act.wait_ge(s_rq, q)
                    nc.scalar.copy(q_p[:, 1, cs], q_rest[:, cs]).then_inc(s_q2, 1)
                    act.wait_ge(s_rk, q)
                    nc.scalar.copy(k_p[:, 1, cs], k_rest[:, cs]).then_inc(s_k2, 1)
            act.wait_ge(st_first, 96)
            for p, made in ((0, s_q1), (1, s_q2)):
                act.wait_ge(made, 4)
                act.dma_start(q_dram[:, p], q_p[:, p, :]).then_inc(l_pieces, 16)
            for half in range(2):
                cs = slice(BT // 2 * half, BT // 2 * (half + 1))
                act.wait_ge(s_k3, 2 + half)
                act.wait_ge(s_q3, 2 + half)
                if half == 1:
                    act.wait_ge(s_last3, 2)
                    act.dma_start(q_dram[:, 2], q_p[:, 2, :]).then_inc(l_pieces, 16)
                act.dma_start(k_dram[:, :, :, cs].rearrange("h d p t -> (h d) p t"), k_p[:, :, cs]).then_inc(l_pieces, 16)

            def slot(it, r):
                e, b = divmod(r, OCT)
                o, S = 2 * it + e, ITER * it + r
                gru = live(S, STEPS)
                if isinstance(o, int) and o in (-5, -4) and b % 2 == 1:
                    q = b // 2
                    bk = extra_bank(o, q)
                    act.wait_ge(s_extra, 4 * (o + 5) + q + 1)
                    if o == -5:
                        nc.scalar.copy(v_all[:, :, 4 * q:4 * q + 4, 0:DH],
                                       bk[:, :].rearrange("p (g h d) -> p h g d", g=4, h=H)).then_inc(s_v, 1)
                    else:
                        nc.scalar.copy(xT[:, :, :, 2 * q:2 * q + 2].rearrange("p i c b -> p b i c"),
                                       bk[:, :].rearrange("p (b i c) -> p b i c", b=2, i=NI)).then_inc(s_xt, 1)
                if gru:
                    act.wait_ge(rn_done, S + 1)
                    nc.scalar.activation(tr[:, :], bN[:, 0:W64], ACT.Tanh, scale=0.5).then_inc(tr_done, 1)
                    act.wait_ge(z_done, S + 1)
                    nc.scalar.activation(tz[:, :], bZ[:, 0:W64], ACT.Tanh, scale=0.5).then_inc(tz_done, 1)
                for g, slot_ev in ((0, 5), (1, 1)):
                    hy = o + LEAD_EXP - g
                    if b == slot_ev and live(hy, H):
                        act.wait_ge(pv_done, 2 * hy + g + 1)
                        at_least(act, yt_done, 2 * hy + g)
                        nc.scalar.copy(yT[:, :], bPV[:, 0:T]).then_inc(yT_done, 1)
                hm = o + LEAD_ROW
                if b == rows_slot(o) + 1 and live(hm, H):
                    act.wait_ge(mxT_done, hm + 1)
                    at_least(act, st_shift[(e + LEAD_ROW + 1) % 2], 16 * (it + (e + LEAD_ROW + 1) // 2))
                    nc.scalar.copy(mx_rows[:, :], bX[:, :].bitcast(BF16)[0:3 * B * NI, 0:128]).then_inc(mxrow_done, 1)
                if b == 0 and live(o - 2, H):
                    rows_out(o - 2, e, it - 1)
                gp = it + 1
                if r == ITER - 1 and live(gp, STEPS // ITER):
                    at_least(act, gib_done, 2 * gp + 1)
                    at_least(act, sel_done, ITER * gp)
                    nc.scalar.copy(gi_cur[:, 0:2, :], gi_next[:, 0:2, :]).then_inc(gicur_done, 1)
                if gru:
                    act.wait_ge(npre_done, S + 1)
                    nc.scalar.activation(h_mul[:, :, 1].rearrange("p (i b) -> p i b", i=NI), n_pre[:, :, :],
                                         ACT.Tanh).then_inc(nt_done, 1)
                if r == ITER - 1 and live(gp, STEPS // ITER):
                    act.wait_ge(gin_mm_done, gp + 1)
                    at_least(act, npre_done, ITER * gp)
                    if isinstance(it, int) and it == -1:
                        act.wait_ge(l_bias, 16 * (2 + NJ))
                    for i in range(NI):
                        nc.scalar.activation(gin_cur[:, i, :, :].rearrange("p s b -> p (s b)"), bGn[:, 128 * i:128 * (i + 1)],
                                             ACT.Identity, bias=bias_n[:, i:i + 1]).then_inc(gin_done, 1)
                hp = o + LEAD_EXP
                if live(hp, H):
                    g, jj = divmod(b, GRP)
                    act.wait_ge(s2_done, B * hp + b + 1)
                    if jj == 0:
                        at_least(act, pv_done, 2 * (hp - 1) + g + 1)
                    nc.scalar.activation(probs[:, g, jj, :], score_bank(S, b % 2, bS2, bZ)[:, :], ACT.Exp, scale=SCALE).then_inc(exp_done, 1)

            def rows_out(o, par, before):
                act.wait_ge(outT_done, o + 1)
                at_least(act, st_out[par], 16 * before)
                nc.scalar.copy(o_sb[:, par, :].rearrange("p (j i f) -> p i j f", j=NJ, i=NI),
                               bX[:, 0:T].rearrange("p (i j f) -> p i j f", i=NI, j=NJ)).then_inc(outev_done, 1)

            slots(act, slot)
            rows_out(H - 1, 1, H // 2 - 1)

        @block.vector
        def _(dve):
            dve.memset(h0[:, :], 0.0).then_inc(s_h0z, 1)
            dve.memset(k_stk[0:ROW_T, :, :].bitcast(F32), 0.0).then_inc(s_kfill, 1)
            dve.wait_ge(l_mask8, 32)
            chain = [0]

            def link(ins):
                chain[0] += 1
                ins.then_inc(s_mrow, 1)
                dve.wait_ge(s_mrow, chain[0])

            link(dve.tensor_scalar(m8[:, 0, :], mask8[:, :], 1.0, -NEG, ALU.subtract, ALU.mult))
            link(dve.tensor_reduce(m8s[:, 1:2], m8[:, 0, :], AX.X, ALU.max))
            link(dve.tensor_scalar(m8s[:, 2:3], m8s[:, 0:1], 1.0 / SCALE, None, ALU.mult))
            link(dve.tensor_scalar(m8[:, 1, :], m8[:, 0, :], m8s[:, 1:2], None, ALU.subtract))
            link(dve.scalar_tensor_tensor(out=m8[:, 2, :], in0=mask8[:, :], scalar=m8s[:, 2:3], in1=m8[:, 1, :],
                                          op0=ALU.mult, op1=ALU.add))

            def perm_out(ap):
                return ap.rearrange("p (i j f) -> p i j f", i=NI, j=NJ)

            def perm_in(ap):
                return ap.rearrange("p (j i f) -> p i j f", j=NJ, i=NI)

            link(dve.tensor_copy(perm_out(m8[:, 3, :]), perm_in(m8[:, 2, :])))
            link(dve.tensor_copy(rows8[:, 0, :], m8[:, 3, :]))
            link(dve.tensor_tensor(m8[:, 0, :], m8[:, 3, :], rows8[:, 0, :], ALU.subtract))
            link(dve.tensor_copy(rows8[:, 1, :], m8[:, 0, :]))
            link(dve.tensor_tensor(rows8[:, 2, :], m8[:, 0, :], rows8[:, 1, :], ALU.subtract))
            for k in range(3):
                last = dve.tensor_copy(perm_out(rows8[:, 3 + k, :]), perm_in(mask8[:, :]))
            last.then_inc(s_rows8, 1)

            dve.wait_ge(l_mask, 16)
            for q in range(4):
                cs = slice(512 * q, 512 * (q + 1))
                dve.wait_ge(s_proj, 2 * q + 2)
                for half in range(2):
                    b = 2 * q + half
                    mk = dve.tensor_tensor(perm_out(k_msk[:, T * b:T * (b + 1)]), perm_out((bS2, bZ)[q % 2][:, T * half:T * (half + 1)]),
                                           perm_in(mask_bc[:, T * b:T * (b + 1)]), ALU.mult)
                mk.then_inc(s_km, 1)
                dve.wait_ge(s_q1, q + 1)
                dve.tensor_tensor(q_rest[:, cs], (bS1, bN)[q % 2][:, :], q_p[:, 0, cs], ALU.subtract).then_inc(s_rq, 1)
                dve.wait_ge(s_k1, q + 1)
                dve.tensor_tensor(k_rest[:, cs], k_msk[:, cs], k_p[:, 0, cs], ALU.subtract).then_inc(s_rk, 1)
            for p, rest, second in ((q_p, q_rest, s_q2), (k_p, k_rest, s_k2)):
                dve.wait_ge(second, 4)
                dve.tensor_tensor(p[:, 2, cs], rest[:, cs], p[:, 1, cs], ALU.subtract).then_inc(s_last3, 1)

            def gru_setup():
                dve.wait_ge(l_gw, 16 * 8)
                dve.tensor_scalar(whh[:, :, 2 * T:3 * T], whh[:, :, 2 * T:3 * T], 0.5, None, ALU.mult).then_inc(s_half, 1)
                dve.wait_ge(l_bias, 16 * (2 + NJ))
                bi = bih_bc[:, :].rearrange("p (g j c) -> p g j c", g=3, j=NJ)
                bh = bhh_bc[:, :].rearrange("p (g j c) -> p g j c", g=3, j=NJ)
                bo = bias_gi[:, :, :, :].rearrange("p j g c -> p g j c")
                for g in range(2):
                    dve.tensor_tensor(bo[:, g], bi[:, g], bh[:, g], ALU.add).then_inc(s_bias_gi, 1)
                links = [0]

                def blink(ins):
                    links[0] += 1
                    ins.then_inc(s_bhn, 1)
                    dve.wait_ge(s_bhn, links[0])

                blink(dve.tensor_scalar(bhn_r[:, 0, :], bhh_bc[:, 2 * T:3 * T], 0.5, None, ALU.mult))
                blink(dve.tensor_copy(bhn_p[:, 0, :], bhn_r[:, 0, :]))
                blink(dve.tensor_tensor(bhn_r[:, 1, :], bhn_r[:, 0, :], bhn_p[:, 0, :], ALU.subtract))
                blink(dve.tensor_copy(bhn_p[:, 1, :], bhn_r[:, 1, :]))
                blink(dve.tensor_tensor(bhn_p[:, 2, :], bhn_r[:, 1, :], bhn_p[:, 1, :], ALU.subtract))
                dve.wait_ge(s_ident, 1)
                blink(dve.tensor_scalar(bhn_r[:, 0, :], bhn_p[:, 0, :], ident[:, 0:1], None, ALU.mult))
                blink(dve.scalar_tensor_tensor(out=bhn_r[:, 1, :], in0=bhn_p[:, 1, :], scalar=ident[:, 1:2],
                                               in1=bhn_r[:, 0, :], op0=ALU.mult, op1=ALU.add))
                dve.scalar_tensor_tensor(out=bhn_rows[:, :], in0=bhn_p[:, 2, :], scalar=ident[:, 2:3],
                                         in1=bhn_r[:, 1, :], op0=ALU.mult, op1=ALU.add).then_inc(s_bhn_rows, 1)
                dve.wait_ge(l_h0, 64)
                dve.wait_ge(s_h0z, 1)
                dve.transpose(h0T[:, :, :].rearrange("p i b -> p (i b)"), h0[:, :]).then_inc(s_h0T, 1)
                dve.wait_ge(s_h0T, 1)
                dve.tensor_copy(h_st[:, :, 1].rearrange("p (i b) -> p i b", i=NI), h0T[:, :, 0:B]).then_inc(h_ready, 1)
                dve.wait_ge(s_scan0, 5)

            def slot(it, r):
                e, b = divmod(r, OCT)
                o, S = 2 * it + e, ITER * it + r
                gru = live(S, STEPS)
                if gru:
                    dve.wait_ge(tr_done, S + 1)
                    dve.scalar_tensor_tensor(out=rn[:, :], in0=tr[:, :], scalar=1.0, in1=bN[:, W64:2 * W64],
                                             op0=ALU.add, op1=ALU.mult).then_inc(rn_used, 1)
                    dve.wait_ge(rn_used, S + 1)
                    dve.transpose(rnT[:, :, :].rearrange("p i b -> p (i b)"), rn[:, :]).then_inc(rnT_done, 1)
                    dve.wait_ge(tz_done, S + 1)
                    dve.transpose(tzT[:, :, :].rearrange("p i b -> p (i b)"), tz[:, :]).then_inc(tzT_done, 1)
                    dve.wait_ge(rnT_done, S + 1)
                    if r == 0:
                        at_least(dve, gin_done, 2 * it + 2)
                    dve.tensor_tensor(n_pre[:, :, :], rnT[:, :, 0:B], gin_cur[:, :, r, :], ALU.add).then_inc(npre_done, 1)
                    dve.wait_ge(tzT_done, S + 1)
                    dve.wait_ge(hh_done, S + 1)
                    dve.scalar_tensor_tensor(out=h_add[:, :, 1].rearrange("p (i b) -> p i b", i=NI), in0=tzT[:, :, 0:B], scalar=1.0,
                                             in1=hh[:, :].rearrange("p (i b) -> p i b", i=NI),
                                             op0=ALU.add, op1=ALU.mult).then_inc(zh_done, 1)
                    dve.tensor_scalar(h_add[:, :, 0].rearrange("p (i b) -> p i b", i=NI), tzT[:, :, 0:B], -0.5, 0.5,
                                      ALU.mult, ALU.add).then_inc(omz_done, 1)
                    dve.wait_ge(nt_done, S + 1)
                    dve.wait_ge(zh_done, S + 1)
                    dve.wait_ge(omz_done, S + 1)
                    at_least(dve, oT_done, S)
                    dve.tensor_tensor_scan(h_st[:, :, :].rearrange("p a e -> p (a e)"), h_mul[:, :, :].rearrange("p a e -> p (a e)"),
                                           h_add[:, :, :].rearrange("p a e -> p (a e)"), 0.0, ALU.mult, ALU.add).then_inc(h_ready, 1)
                for g, slot_n in ((0, 6), (1, 2)):
                    hy = o + LEAD_EXP - g
                    if b == slot_n and live(hy, H):
                        yv = bX[:, 0:T].rearrange("p (i b d) -> p i b d", i=NI, b=GRP)
                        dve.wait_ge(yt_done, 2 * hy + g + 1)
                        at_least(dve, x1_done, 2 * hy + g)
                        dve.reciprocal(y_inv[:, :, :], yv[:, :, :, DH]).then_inc(inv_done, 1)
                        dve.wait_ge(inv_done, 2 * hy + g + 1)
                        dve.tensor_tensor(y_n[:, :, :, :], yv[:, :, :, 0:DH],
                                          y_inv[:, :, :].unsqueeze(3).to_broadcast([128, NI, GRP, DH]),
                                          ALU.mult).then_inc(norm_done, 1)
                gp = it + 1
                if r in (12, 13) and live(gp, STEPS // ITER):
                    half = r - 12
                    js = slice(2 * half, 2 * half + 2)
                    dve.wait_ge(gimm_done, 2 * gp + half + 1)
                    part = bG[:, 256 * half:256 * (half + 1)].rearrange("p (j c) -> p j c", j=2)
                    if half == 0:
                        at_least(dve, gicur_done, 2 * gp)
                        dve.tensor_tensor(gi_next[:, js, :], part, bias_gi[:, js, :, :].rearrange("p j g c -> p j (g c)"),
                                          ALU.add).then_inc(gib_done, 1)
                    else:
                        dve.tensor_copy(gi_next[:, js, :], part).then_inc(gib_done, 1)
                hx = o + LEAD_MAX
                if live(hx, H):
                    dve.wait_ge(s1_done, B * hx + b + 1)
                    if b == 0:
                        at_least(dve, split_done, hx - 1)
                    dve.tensor_reduce(neg_max[:, (e + LEAD_MAX) % 2, NI * b:NI * b + NI],
                                      score_bank(S, b % 2, bS1, bN)[:, :].rearrange("p (i k) -> p i k", i=NI), AX.X, ALU.max,
                                      negate=True).then_inc(max_done, 1)

            gru_setup()
            slots(dve, slot)

        @block.tensor
        def _(pe):
            pe.wait_ge(l_w, 48)
            pe.wait_ge(s_ident, 1)
            for n in range(3):
                last = nc.tensor.transpose(bX[:, C * n:C * (n + 1)], w_nat[:, n, :], ident[:, :])
            last.then_inc(s_wt, 1)
            pe.wait_ge(s_wT, 1)
            for q in range(4):
                cs = slice(512 * q, 512 * (q + 1))
                pe.wait_ge(s_xp, 2 * (q + 1))
                at_least(pe, s_rq, q - 1)
                nc.tensor.matmul((bS1, bN)[q % 2][:, :], wT[:, 0, :], xp[:, cs], start=True, stop=True).then_inc(s_proj, 1)
                at_least(pe, s_km, q - 1)
                nc.tensor.matmul((bS2, bZ)[q % 2][:, :], wT[:, 1, :], xp[:, cs], start=True, stop=True).then_inc(s_proj, 1)
            pe.wait_ge(s_sel, 1)
            pe.wait_ge(s_identb, 1)
            pe.wait_ge(s_fill, 5)
            pe.wait_ge(s_scan0, 5)
            pe.wait_ge(s_rq, 4)
            pe.wait_ge(s_km, 4)

            def hidden(bk, first, n):
                for i in range(NI):
                    for j in range(NJ):
                        w = whh[:, i, :].rearrange("p (g j c) -> p j g c", g=3, j=NJ)[:, j, first:first + 2 * n - 1:2]
                        last = nc.tensor.matmul(bk[32 * j:32 * j + B, 0:n * W64], h_st[:, B * i:B * (i + 1), 1], w,
                                                start=False, stop=(i == NI - 1), skip_group_check=True)
                return last

            def given(bk, s, g):
                for j in range(NJ):
                    last = nc.tensor.matmul(bk[32 * j:32 * j + 32, 0:W64], sel[:, s, :],
                                            gi_cur[:, j, W64 * g:W64 * (g + 1)],
                                            start=True, stop=False, skip_group_check=True)
                return last

            def slot(it, r):
                e, b = divmod(r, OCT)
                o, S = 2 * it + e, ITER * it + r
                if live(S, STEPS):
                    pe.wait_ge(h_ready, S + 1)
                    hidden(bN, 0, 2).then_inc(rn_done, 1)
                    hidden(bZ, 1, 1).then_inc(z_done, 1)
                ahead = live(S + 1, STEPS)
                s = (r + 1) % ITER
                if isinstance(it, int) and it == -1 and r == ITER - 1:
                    pe.wait_ge(max_done, B * LEAD_MAX - 1)
                    pe.wait_ge(exp_done, B * LEAD_EXP - 1)
                    pe.wait_ge(s_bhn_rows, 1)
                    pe.wait_ge(s_half, 1)
                hx = o + LEAD_MAX
                if live(hx, H):
                    par = (e + LEAD_MAX) % 2
                    if isinstance(hx, int) and hx == 0 and b == 0:
                        pe.wait_ge(st_first, 96)
                        pe.wait_ge(st_mask, 32)
                    if b == (4 if isinstance(hx, int) and hx == 0 else 0):
                        pe.wait_ge(st1[par], 2 * 16 * (it + (e + LEAD_MAX) // 2 + 1 + 2 * (1 - par)))
                    at_least(pe, max_done, free_below(S, B * hx + b))
                    qs, ks = stk1[par]
                    for i in range(NI):
                        last = nc.tensor.matmul(score_bank(S, b % 2, bS1, bN)[:, T * i:T * (i + 1)], qs[0:ROW_M, T * b + 128 * i:T * b + 128 * (i + 1)],
                                                ks[0:ROW_M, T * b:T * (b + 1)], start=True, stop=True)
                    last.then_inc(s1_done, 1)
                if ahead and r < ITER - 1:
                    prepare(it, r, s, S)
                if isinstance(o, int) and o in (-5, -4):
                    extra(o, b)
                hp = o + LEAD_EXP
                if live(hp, H):
                    par = (e + LEAD_EXP) % 2
                    if b == 0:
                        n_th = it + (e + LEAD_EXP) // 2 + 1
                        pe.wait_ge(st2[par], 2 * 16 * n_th)
                        pe.wait_ge(st_shift[par], 16 * n_th)
                    at_least(pe, exp_done, free_below(S, B * hp + b))
                    qs, ks = stk2[par]
                    for i in range(NI):
                        last = nc.tensor.matmul(score_bank(S, b % 2, bS2, bZ)[:, T * i:T * (i + 1)], ks[0:NROW, T * b + 128 * i:T * b + 128 * (i + 1)],
                                                qs[0:NROW, T * b:T * (b + 1)], start=True, stop=True)
                    last.then_inc(s2_done, 1)
                for g, slot_pv in ((0, 4), (1, 0)):
                    hy = o + LEAD_EXP - g
                    if b == slot_pv and live(hy, H):
                        if isinstance(hy, int) and hy == 0 and g == 0:
                            pe.wait_ge(s_xt, 4)
                        pe.wait_ge(exp_done, B * hy + GRP * (g + 1))
                        pe.wait_ge(vcur_done, hy + 1)
                        at_least(pe, yT_done, 2 * hy + g)
                        for i in range(NI):
                            for jj in range(GRP):
                                last = nc.tensor.matmul(bPV[32 * jj:32 * jj + 32, 0:T], v_cur[:, NI * (GRP * g + jj) + i, :],
                                                        probs[:, g, jj, T * i:T * (i + 1)],
                                                        start=(i == 0), stop=(i == NI - 1), skip_group_check=True)
                        last.then_inc(pv_done, 1)
                    if b == slot_pv + 1 and live(hy, H):
                        pe.wait_ge(yT_done, 2 * hy + g + 1)
                        if g == 0:
                            at_least(pe, mxrow_done, o + LEAD_ROW + 1, H)
                        else:
                            at_least(pe, outev_done, o - 1)
                            at_least(pe, norm_done, 2 * hy + 1)
                        for i in range(NI):
                            last = nc.tensor.transpose(bX[:, 128 * i:128 * (i + 1)], yT[:, 128 * i:128 * (i + 1)], ident[:, :])
                        last.then_inc(yt_done, 1)
                hm = o + LEAD_ROW
                if b == rows_slot(o) and live(hm, H):
                    pe.wait_ge(split_done, hm + 1)
                    at_least(pe, norm_done, 2 * (o + LEAD_EXP))
                    nc.tensor.transpose(bX[:, :].bitcast(BF16)[:, 0:128],
                                        mx_p[:, :, :].rearrange("p n a -> p (n a)"), identb[:, :]).then_inc(mxT_done, 1)
                gp = it + 1
                if r in (11, 12) and live(gp, STEPS // ITER):
                    half = r - 11
                    at_least(pe, x1cur_done, 4 * (gp + 1))
                    if isinstance(it, int) and it == -1:
                        pe.wait_ge(l_gw, 128)
                    at_least(pe, gib_done, 2 * gp + half)
                    for j in range(2 * half, 2 * half + 2):
                        for i in range(NI):
                            last = nc.tensor.matmul(bG[:, 128 * j:128 * (j + 1)], x1_cur[:, i, :, :, :].rearrange("p a c b -> p (a c b)"),
                                                    wih[:, i, :].rearrange("p (g j c) -> p j g c", g=3, j=NJ)[:, j, 0:2],
                                                    start=(i == 0), stop=(i == NI - 1))
                    last.then_inc(gimm_done, 1)
                if r == 13 and live(gp, STEPS // ITER):
                    at_least(pe, gin_done, NI * gp)
                    if isinstance(it, int) and it == -1:
                        pe.wait_ge(s_wihn, NI)
                    for io in range(NI):
                        for i in range(NI):
                            last = nc.tensor.matmul(bGn[:, 128 * io:128 * (io + 1)], wih_n[:, i, io, :],
                                                    x1_cur[:, i, :, :, :].rearrange("p a c b -> p (a c b)"),
                                                    start=(i == 0), stop=(i == NI - 1))
                    last.then_inc(gin_mm_done, 1)
                if b == OCT - 1 and live(o - 1, H):
                    transpose_out(o - 1, (e + 1) % 2)
                if ahead and r == ITER - 1:
                    prepare(it, r, s, S)

            def extra(o, b):
                q, second = divmod(b, 2)
                bk = extra_bank(o, q)
                if second == 0:
                    if o == -5:
                        at_least(pe, s_v, q - 2)
                    else:
                        at_least(pe, s_v, q + 2, 4)
                        at_least(pe, s_xt, q - 2)
                for g in (2 * second, 2 * second + 1):
                    blk = xp[:, 512 * q + 128 * g:512 * q + 128 * (g + 1)]
                    if o == -5:
                        last = nc.tensor.matmul(bk[:, 128 * g:128 * (g + 1)], blk, wT[:, 2, :], start=True, stop=True)
                    else:
                        last = nc.tensor.transpose(bk[:, 128 * g:128 * (g + 1)], blk, ident[:, :])
                if second == 1:
                    last.then_inc(s_extra, 1)

            def prepare(it, r, s, S):
                if r == ITER - 1:
                    pe.wait_ge(gicur_done, 2 * (it + 1) + 2)
                at_least(pe, rn_used, S + 1)
                given(bN, s, 0)
                for j in range(NJ):
                    nc.tensor.matmul(bN[32 * j:32 * j + 32, W64:2 * W64], ones_rows[:, :], bhn_rows[:, W64 * j:W64 * (j + 1)],
                                     start=False, stop=False, skip_group_check=True)
                at_least(pe, tz_done, S + 1)
                given(bZ, s, 1).then_inc(sel_done, 1)

            def transpose_out(o, par):
                pe.wait_ge(oT_done, OCT * (o + 1))
                at_least(pe, outev_done, o)
                at_least(pe, norm_done, 2 * (o + 1 + LEAD_EXP) + 1, 2 * H)
                for i in range(NI):
                    last = nc.tensor.transpose(bX[:, 128 * i:128 * (i + 1)], oT[:, par, i, :], ident[:, :])
                last.then_inc(outT_done, 1)

            slots(pe, slot)


_INS = ['x', 'cond_2048', 'L0_cond_Wq', 'L0_cond_Wk', 'L0_cond_Wv', 'L0_cond_b',
        'L1_cond_W_ih', 'L1_cond_W_hh', 'L1_cond_b_ih', 'L1_cond_b_hh']


def kernel(**inputs):
    import numpy as np
    import concourse.bacc as bacc
    from concourse.bass_utils import run_bass_kernel_spmd

    nc = bacc.Bacc("TRN2", target_bir_lowering=False, num_devices=1)
    arrays, args = {}, []
    for name in _INS:
        a = np.ascontiguousarray(inputs[name])
        arrays[f"in_{name}"] = a
        args.append(nc.dram_tensor(f"in_{name}", a.shape, mybir.dt.from_np(a.dtype), kind="ExternalInput").ap())
    out = nc.dram_tensor("out_x", [B, C, T], F32, kind="ExternalOutput").ap()
    build(nc, *args, out)
    r = run_bass_kernel_spmd(nc, [arrays], core_ids=[0])
    return r.results[0]["out_x"]
```

```python
from contextlib import ExitStack

import concourse.bass as bass
from concourse import mybir

F32 = mybir.dt.float32
BF16 = mybir.dt.bfloat16
ACT = mybir.ActivationFunctionType
ALU = mybir.AluOpType
AX = mybir.AxisListType

B = 8
C = 128
T = 256
H = 16
DH = C // H
NI = T // 128
NJ = 4
W64 = T // NJ
BT = B * T
OCT = 8
ITER = 2 * OCT
STEPS = C
GRP = 4
EXT = DH + 1
LEAD_MAX, LEAD_ROW, LEAD_EXP = 5, 4, 3
TERMS = 9 * DH
ROW_T = 32
ROW_M = ROW_T + TERMS
NROW = ROW_M + 3
SCALE = float(DH) ** -0.5
NEG = -1e30 / SCALE


def live(n, end):
    return not isinstance(n, int) or 0 <= n < end


def at_least(eng, sem, n, most=1 << 20):
    if isinstance(n, int):
        if n <= 0:
            return
        n = min(n, most)
    eng.wait_ge(sem, n)


def build(nc, x, mask, Wq, Wk, Wv, att_b, W_ih, W_hh, b_ih, b_hh, out):
    with ExitStack() as ctx:
        def sb(name, shape, dt=F32):
            return ctx.enter_context(nc.sbuf_tensor(name, shape, dt))

        def bank(name):
            return ctx.enter_context(nc.psum_tensor(name, [128, 512], F32))

        def sem(name):
            return ctx.enter_context(nc.semaphore(name))

        q_dram = nc.dram_tensor("q_pieces", [H, 3, DH, BT], BF16).ap()
        k_dram = nc.dram_tensor("k_pieces", [H, DH, 3, BT], BF16).ap()
        row_dram = nc.dram_tensor("mask_rows", [6, BT], BF16).ap()

        x_sb = sb("x_sb", [C, BT])
        xp = sb("xp", [C, BT])
        mask_bc = sb("mask_bc", [C, BT])
        w_nat = sb("w_nat", [C, 3, C])
        wT = sb("wT", [C, 3, C])
        wih = sb("wih", [128, NI, 3 * T])
        wih_n = sb("wih_n", [128, NI, NI, 128])
        whh = sb("whh", [128, NI, 3 * T])
        bih_bc = sb("bih_bc", [128, 3 * T])
        bhh_bc = sb("bhh_bc", [128, 3 * T])
        bias_gi = sb("bias_gi", [128, NJ, 2, W64])
        bias_n = sb("bias_n", [128, NI])
        bhn_p = sb("bhn_p", [128, 3, T], BF16)
        bhn_r = sb("bhn_r", [128, 2, T])
        bhn_rows = sb("bhn_rows", [128, T], BF16)
        ones_rows = sb("ones_rows", [128, 32], BF16)
        ident = sb("ident", [128, 128])
        identb = sb("identb", [128, 128], BF16)
        sel = sb("sel", [128, ITER, 32])
        mask8 = sb("mask8", [B, T])
        m8 = sb("m8", [B, 4, T])
        m8s = sb("m8s", [B, 4])
        rows8 = sb("rows8", [B, 6, T], BF16)
        q_p = sb("q_p", [C, 3, BT], BF16)
        k_p = sb("k_p", [C, 3, BT], BF16)
        q_rest = sb("q_rest", [C, BT])
        k_msk = sb("k_msk", [C, BT])
        k_rest = sb("k_rest", [C, BT])
        v_all = sb("v_all", [128, H, B * NI, EXT])
        xT = sb("xT", [128, NI, C, B])

        q_stk = sb("q_stk", [128, 4, BT], BF16)
        k_stk = sb("k_stk", [128, 4, BT], BF16)
        stk1 = [[t[:, par, :] for t in (q_stk, k_stk)] for par in range(2)]
        stk2 = [[t[:, 2 + par, :] for t in (q_stk, k_stk)] for par in range(2)]
        neg_max = sb("neg_max", [128, 2, B * NI])
        mx_p = sb("mx_p", [128, 8, B * NI], BF16)
        mx_r = sb("mx_r", [128, 2, B * NI])
        zero16 = sb("zero16", [128, NI * B])
        half16 = sb("half16", [128, NI * B])
        table_dummy = sb("table_dummy", [128, 1])
        carrier = sb("carrier", [128, 1])
        mx_rows = sb("mx_rows", [3 * B * NI, 128], BF16)
        v_cur = sb("v_cur", [128, B * NI, 32])
        probs = sb("probs", [128, 2, GRP, NI * T])
        yT = sb("yT", [128, T])
        y_inv = sb("y_inv", [128, NI, GRP])
        y_n = sb("y_n", [128, NI, GRP, DH])
        x1_cur = sb("x1_cur", [128, NI, 2, DH, B])
        gi_cur = sb("gi_cur", [128, NJ, 2 * W64])
        gin_cur = sb("gin_cur", [128, NI, ITER, B])

        h0 = sb("h0", [128, W64])
        h0T = sb("h0T", [128, NI, 32])
        tr = sb("tr", [128, W64])
        tz = sb("tz", [128, W64])
        tzT = sb("tzT", [128, NI, 32])
        hh = sb("hh", [128, NI * B])
        rn = sb("rn", [128, W64])
        rnT = sb("rnT", [128, NI, 32])
        n_pre = sb("n_pre", [128, NI, B])
        h_mul = sb("h_mul", [128, NI * B, 2])
        h_add = sb("h_add", [128, NI * B, 2])
        h_st = sb("h_st", [128, NI * B, 2])
        oT = sb("oT", [128, 2, NI, 128])
        o_sb = sb("o_sb", [128, 2, T])

        bN, bZ = bank("bN"), bank("bZ")
        bS1, bS2 = bank("bS1"), bank("bS2")
        bPV, bX = bank("bPV"), bank("bX")
        bG, bGn = bank("bG"), bank("bGn")

        l_x = [sem(f"l_x{q}") for q in range(4)]
        l_w, l_mask, l_mask8 = sem("l_w"), sem("l_mask"), sem("l_mask8")
        l_gw, l_bias, l_h0 = sem("l_gw"), sem("l_bias"), sem("l_h0")
        l_rows, l_pieces = sem("l_rows"), sem("l_pieces")
        s_h0z, s_pool0, s_ident, s_identb, s_sel = sem("s_h0z"), sem("s_pool0"), sem("s_ident"), sem("s_identb"), sem("s_sel")
        s_fill, s_stkfill, s_kfill, s_tables = sem("s_fill"), sem("s_stkfill"), sem("s_kfill"), sem("s_tables")
        s_mrow, s_bhn, s_rows8 = sem("s_mrow"), sem("s_bhn"), sem("s_rows8")
        s_bhn_rows, s_bias_gi, s_half = sem("s_bhn_rows"), sem("s_bias_gi"), sem("s_half")
        s_wt, s_wT = sem("s_wt"), sem("s_wT")
        s_xp = sem("s_xp")
        s_proj, s_q1, s_rq, s_km, s_k1, s_rk, s_k2 = [sem(n) for n in (
            "s_proj", "s_q1", "s_rq", "s_km", "s_k1", "s_rk", "s_k2")]
        s_q2, s_q3, s_k3, s_last3, s_vproj, s_turned, s_v, s_xt = [sem(n) for n in ("s_q2", "s_q3", "s_k3", "s_last3", "s_vproj", "s_turned", "s_v", "s_xt")]
        st1 = [sem(f"st1_{p}") for p in range(2)]
        st_first, st_mask = sem("st_first"), sem("st_mask")
        st2 = [sem(f"st2_{p}") for p in range(2)]
        st_shift = [sem(f"st_shift{p}") for p in range(2)]
        s1_done, max_done, split_step, split_done = sem("s1_done"), sem("max_done"), sem("split_step"), sem("split_done")
        mxT_done, mxrow_done = sem("mxT_done"), sem("mxrow_done")
        s2_done, exp_done, vcur_done, pv_done = sem("s2_done"), sem("exp_done"), sem("vcur_done"), sem("pv_done")
        yT_done, yt_done, inv_done, norm_done = sem("yT_done"), sem("yt_done"), sem("inv_done"), sem("norm_done")
        x1_done, x1cur_done = sem("x1_done"), sem("x1cur_done")
        gimm_done, gicur_done, sel_done = sem("gimm_done"), sem("gicur_done"), sem("sel_done")
        rn_done, z_done = sem("rn_done"), sem("z_done")
        tr_done, tz_done, nt_done = sem("tr_done"), sem("tz_done"), sem("nt_done")
        rn_used, rnT_done, tzT_done = sem("rn_used"), sem("rnT_done"), sem("tzT_done")
        npre_done, zh_done, omz_done = sem("npre_done"), sem("zh_done"), sem("omz_done")
        h_ready, hh_done = sem("h_ready"), sem("hh_done")
        s_h0T, s_scan0, s_wihn = sem("s_h0T"), sem("s_scan0"), sem("s_wihn")
        gin_mm_done, gin_done = sem("gin_mm_done"), sem("gin_done")
        oT_done, outT_done, outev_done = sem("oT_done"), sem("outT_done"), sem("outev_done")
        st_out = [sem(f"st_out{p}") for p in range(2)]

        spare = (bPV, bG, bGn, bX)

        def rows_slot(o):
            return 2 if isinstance(o, int) and o < -2 else 4

        def score_bank(S, odd, bk, other):
            return other if isinstance(S, int) and S < -2 and odd else bk

        def free_below(S, n):
            return n - 1 if isinstance(S, int) and S < -2 else n

        def slots(eng, slot):
            for it in range(-3, 1):
                for r in range(ITER):
                    slot(it, r)
            full = (H - LEAD_MAX - 1) // 2
            with eng.Fori(1, full) as it:
                for r in range(ITER):
                    slot(it, r)
            for it in range(full, STEPS // ITER):
                for r in range(ITER):
                    slot(it, r)
            for r in range(OCT):
                slot(STEPS // ITER, r)

        block = ctx.enter_context(nc.Block())

        @block.sync
        def _(sp):
            xv = x.rearrange("b c t -> c b t")
            x_v = x_sb[:, :].rearrange("c (b t) -> c b t", b=B)
            for q in range(4):
                sp.dma_start(x_v[:, 2 * q:2 * q + 2, :], xv[:, 2 * q:2 * q + 2, :]).then_inc(l_x[q], 16)
            for j in range(NJ):
                sp.dma_start(bias_n[32 * j:32 * j + 32, :],
                             b_ih.rearrange("(g j i f) -> g j f i", g=3, j=NJ, i=NI)[2, j],
                             allow_slow_non_contiguous=True).then_inc(l_bias, 16)
            sp.dma_start(mask_bc[:, :], mask.rearrange("b t -> (b t)").partition_broadcast(C)).then_inc(l_mask, 16)
            sp.wait_ge(s_h0z, 1)
            sp.wait_ge(s_tables, 1)
            for j in range(NJ):
                sp.dma_start(h0[32 * j:32 * j + B, :], mask[:, W64 * j:W64 * (j + 1)]).then_inc(l_h0, 16)
            for w, dst in ((W_ih, wih), (W_hh, whh)):
                wv = w.rearrange("(j i f) n -> j f i n", j=NJ, i=NI)
                for j in range(NJ):
                    sp.dma_start(dst[32 * j:32 * j + 32, :, :], wv[j]).then_inc(l_gw, 16)
            sp.wait_ge(s_rows8, 1)
            sp.dma_start(row_dram.rearrange("r (b t) -> b r t", b=B), rows8[:, :, :]).then_inc(l_rows, 16)
            sp.wait_ge(l_rows, 16)
            sp.wait_ge(s_kfill, 1)
            sp.dma_start(k_stk[0:3, :, :], row_dram[0:3].unsqueeze(1).to_broadcast([3, 4, BT])).then_inc(st_mask, 16)
            sp.dma_start(k_stk[ROW_M:NROW, 2:4, :], row_dram[3:6].unsqueeze(1).to_broadcast([3, 2, BT])).then_inc(st_mask, 16)

            def load_stack(stk, at, h_):
                sp.dma_start(stk[0][ROW_T:ROW_M, :], q_dram[bass.ds(h_, 1)].rearrange("h p d t -> (h p d) t").unsqueeze(1).to_broadcast([3 * DH, 3, BT])).then_inc(at, 16)
                sp.dma_start(stk[1][ROW_T:ROW_M, :], k_dram[bass.ds(h_, 1)].rearrange("h d p t -> h (d p) t").to_broadcast([3, 3 * DH, BT])).then_inc(at, 16)

            for half, at in ((0, st_first), (1, st1[0])):
                sp.wait_ge(s_k3, 2 + half)
                if half == 1:
                    sp.wait_ge(s_last3, 2)
                cs = slice(BT // 2 * half, BT // 2 * (half + 1))
                for p in range(3):
                    rows = slice(ROW_T + 3 * DH * p, ROW_T + 3 * DH * (p + 1))
                    sp.dma_start(stk1[0][0][rows, cs], q_p[0:DH, p:p + 1, cs].to_broadcast([DH, 3, BT // 2])).then_inc(at, 16)
                    sp.dma_start(stk1[0][1][rows, cs], k_p[0:DH, :, cs]).then_inc(at, 16)
            sp.wait_ge(l_pieces, 64)
            load_stack(stk1[1], st1[1], 1)
            for h_ in range(2):
                load_stack(stk2[h_], st2[h_], h_)

            def slot(it, r):
                e, b = divmod(r, OCT)
                o = 2 * it + e
                if b == 0:
                    if live(o + LEAD_MAX - 1, H - 2):
                        at_least(sp, s1_done, B * (o + LEAD_MAX))
                        par = (e + LEAD_MAX + 1) % 2
                        load_stack(stk1[par], st1[par], o + LEAD_MAX + 1)
                    if live(o + LEAD_EXP - 1, H - 2):
                        at_least(sp, s2_done, B * (o + LEAD_EXP))
                        par = (e + LEAD_EXP + 1) % 2
                        load_stack(stk2[par], st2[par], o + LEAD_EXP + 1)
                if b == rows_slot(o) + 1 and live(o + LEAD_ROW, H):
                    par = (e + LEAD_ROW) % 2
                    at_least(sp, mxrow_done, o + LEAD_ROW + 1)
                    sp.dma_start(stk2[par][0][ROW_M:NROW, :].rearrange("p (a t) -> p a t", a=B * NI),
                                 mx_rows[:, :]).then_inc(st_shift[par], 16)
                if b == 5 and live(o - 1, H):
                    at_least(sp, outev_done, o)
                    sp.dma_start(out[:, bass.ds((o - 1) * OCT, OCT), :].rearrange("b c t -> c b t"),
                                 o_sb[0:OCT * B, (e + 1) % 2, :]).then_inc(st_out[(e + 1) % 2], 16)

            slots(sp, slot)
            for par in range(2):
                sp.wait_ge(st_out[par], 16 * H // 2)

        @block.gpsimd
        def _(pool):
            pool.memset(ident[:, :], 0.0).then_inc(s_pool0, 1)
            pool.wait_ge(s_pool0, 1)
            pool.affine_select(out=ident[:, :], in_=ident[:, :], compare_op=ALU.not_equal, fill=1.0, base=0,
                               pattern=[[-1, 128]], channel_multiplier=1).then_inc(s_ident, 1)
            pool.wait_ge(s_ident, 1)
            pool.tensor_copy(identb[:, :], ident[:, :]).then_inc(s_identb, 1)
            pool.memset(sel[:, :, :], 0.0).then_inc(s_pool0, 1)
            pool.wait_ge(s_pool0, 2)
            pool.tensor_copy(sel[:, :, 0:B], ident[:, :].rearrange("p (s b) -> p s b", b=B)).then_inc(s_sel, 1)
            pool.memset(h_mul[:, :, :], 0.0).then_inc(s_scan0, 1)
            pool.memset(oT[:, :, :, :], 0.0).then_inc(s_scan0, 1)
            pool.memset(zero16[:, :], 0.0).then_inc(s_scan0, 1)
            pool.memset(half16[:, :], 0.5).then_inc(s_scan0, 1)
            pool.memset(mx_p[:, :, :], 0.0).then_inc(s_scan0, 1)
            pool.memset(v_cur[:, :, :], 0.0).then_inc(s_fill, 1)
            pool.memset(v_all[:, :, :, DH:EXT], 1.0).then_inc(s_fill, 1)
            pool.memset(ones_rows[:, :], 0.0).then_inc(s_fill, 1)
            pool.wait_ge(s_fill, 3)
            pool.memset(ones_rows[0:3, :], 1.0).then_inc(s_fill, 1)
            pool.memset(q_stk[0:ROW_T, :, :].bitcast(F32), 0.0).then_inc(s_stkfill, 1)
            pool.wait_ge(s_stkfill, 1)
            pool.memset(q_stk[0:3, :, :], 1.0).then_inc(s_fill, 1)
            for q in range(3):
                cs = slice(512 * q, 512 * (q + 1))
                pool.wait_ge(s_q2, q + 1)
                pool.tensor_tensor(q_p[:, 2, cs], q_rest[:, cs], q_p[:, 1, cs], ALU.subtract).then_inc(s_q3, 1)
                pool.wait_ge(s_k2, q + 1)
                pool.tensor_tensor(k_p[:, 2, cs], k_rest[:, cs], k_p[:, 1, cs], ALU.subtract).then_inc(s_k3, 1)

            for p, made in ((0, s_q1), (1, s_q2)):
                pool.wait_ge(made, 4)
                pool.dma_start(q_dram[:, p], q_p[:, p, :]).then_inc(l_pieces, 16)
            pool.wait_ge(s_q3, 3)
            pool.wait_ge(s_k3, 3)
            pool.wait_ge(s_last3, 2)
            pool.dma_start(q_dram[:, 2], q_p[:, 2, :]).then_inc(l_pieces, 16)
            pool.dma_start(k_dram.rearrange("h d p t -> (h d) p t"), k_p[:, :, :]).then_inc(l_pieces, 16)

            def zeros(*dims):
                return zero16[:, 0:1].rearrange("p (a b c) -> p a b c", a=1, b=1).to_broadcast([128, *dims])

            pool.wait_ge(l_gw, 128)
            for i in range(NI):
                pool.tensor_copy(wih_n[:, i, :, :].rearrange("p a (j f) -> p a j f", j=NJ),
                                 wih[:, i, 2 * T:3 * T].rearrange("p (j a f) -> p a j f", j=NJ, a=NI)).then_inc(s_wihn, 1)
            pool.wait_ge(s_scan0, 5)

            def slot(it, r):
                e, b = divmod(r, OCT)
                o, S = 2 * it + e, ITER * it + r
                if live(S, STEPS):
                    at_least(pool, h_ready, S + 1)
                    pool.tensor_tensor(hh[:, :], h_st[:, :, 1], half16[:, :], ALU.mult).then_inc(hh_done, 1)
                hm = o + LEAD_ROW
                if b == 0 and live(hm, H):
                    nm = neg_max[:, (e + LEAD_ROW) % 2, :]
                    at_least(pool, max_done, B * (hm + 1))
                    at_least(pool, mxT_done, hm)
                    pool.tensor_tensor(mx_p[:, 0, :], nm, zero16[:, :], ALU.add).then_inc(split_step, 1)
                    pool.wait_ge(split_step, 4 * hm + 1)
                    pool.tensor_tensor(mx_r[:, 0, :], nm, mx_p[:, 0, :], ALU.subtract).then_inc(split_step, 1)
                    pool.wait_ge(split_step, 4 * hm + 2)
                    pool.tensor_tensor(mx_p[:, 1, :], mx_r[:, 0, :], zero16[:, :], ALU.add).then_inc(split_step, 1)
                    pool.wait_ge(split_step, 4 * hm + 3)
                    pool.tensor_tensor(mx_r[:, 1, :], mx_r[:, 0, :], mx_p[:, 1, :], ALU.subtract).then_inc(split_step, 1)
                    pool.wait_ge(split_step, 4 * hm + 4)
                    pool.tensor_tensor(mx_p[:, 2, :], mx_r[:, 1, :], zero16[:, :], ALU.add).then_inc(split_done, 1)
                hv = o + LEAD_EXP
                if b == 2 and live(hv, H):
                    at_least(pool, pv_done, 2 * hv)
                    if isinstance(hv, int) and hv == 0:
                        pool.wait_ge(s_v, 4)
                        pool.wait_ge(s_fill, 4)
                    pool.tensor_tensor(v_cur[:, :, 0:EXT].unsqueeze(1), v_all[:, bass.ds(hv, 1), :, :], zeros(1, B * NI, EXT), ALU.add).then_inc(vcur_done, 1)
                for g, slot_add in ((0, 0), (1, 3)):
                    hy = o + LEAD_EXP - 1
                    if b == slot_add and live(hy, H):
                        rows = slice(GRP * g, GRP * g + GRP)
                        at_least(pool, norm_done, 2 * hy + g + 1)
                        if isinstance(hy, int) and hy == 0:
                            pool.wait_ge(s_xt, 4)
                        xv = xT[:, :, bass.ds(hy * DH, DH), rows].rearrange("p i c b -> p i b c")
                        pool.tensor_tensor(xv, y_n[:, :, :, :], xv, ALU.add).then_inc(x1_done, 1)
                if b in (1, 3) and live(o + LEAD_EXP - 1, H):
                    add_current(it, e, b // 3, o + LEAD_EXP - 1)
                if live(S, STEPS):
                    if b == 0:
                        at_least(pool, outT_done, o - 1)
                        at_least(pool, x1_done, 2 * o + 2)
                    at_least(pool, h_ready, S + 2)
                    pool.tensor_tensor(oT[:, e, :, B * b:B * (b + 1)], h_st[:, :, 1].rearrange("p (i b) -> p i b", i=NI),
                                       xT[:, :, bass.ds(S, 1), :].rearrange("p i c b -> p i (c b)"), ALU.add).then_inc(oT_done, 1)

            def add_current(it, e, g, hy):
                chans = bass.ds(hy * DH, DH)
                rows = slice(GRP * g, GRP * g + GRP)
                at_least(pool, x1_done, 2 * hy + g + 1)
                par = (e + LEAD_EXP - 1) % 2
                at_least(pool, gin_mm_done, it + (e + LEAD_EXP - 1) // 2)
                pool.tensor_tensor(carrier[:, :], half16[:, 0:1], half16[:, 0:1], ALU.add)
                pool.tensor_tensor(x1_cur[:, :, par, :, rows], xT[:, :, chans, rows], zeros(NI, DH, GRP), ALU.add).then_inc(x1cur_done, 1)

            slots(pool, slot)

        @block.scalar
        def _(act):
            for n, w in enumerate((Wq, Wk, Wv)):
                act.dma_start(w_nat[:, n, :], w).then_inc(l_w, 16)
            act.wait_ge(s_h0z, 1)
            nc.scalar.activation(table_dummy[:, :], h0[:, 0:1], ACT.Exp).then_inc(s_tables, 1)
            act.dma_start(mask8[:, :], mask).then_inc(l_mask8, 16)
            act.dma_start(m8s[:, 0:1], att_b.partition_broadcast(B)).then_inc(l_mask8, 16)
            act.dma_start(bih_bc[:, :], b_ih.partition_broadcast(128)).then_inc(l_bias, 16)
            act.dma_start(bhh_bc[:, :], b_hh.partition_broadcast(128)).then_inc(l_bias, 16)
            act.wait_ge(s_wt, 1)
            nc.scalar.copy(wT[:, :, :], bX[:, 0:3 * C].rearrange("p (n o) -> p n o", n=3)).then_inc(s_wT, 1)
            for b in range(B):
                act.wait_ge(l_x[b // 2], 16)
                nc.scalar.copy(xp[:, T * b:T * (b + 1)].rearrange("p (i j f) -> p i j f", i=NI, j=NJ),
                               x_sb[:, T * b:T * (b + 1)].rearrange("p (j i f) -> p i j f", j=NJ, i=NI)).then_inc(s_xp, 1)
            for q in range(5):
                if q < 4:
                    cs = slice(512 * q, 512 * (q + 1))
                    act.wait_ge(s_proj, 2 * q + 1)
                    nc.scalar.copy(q_p[:, 0, cs], (bS1, bN)[q % 2][:, :]).then_inc(s_q1, 1)
                    act.wait_ge(s_km, q + 1)
                    nc.scalar.copy(k_p[:, 0, cs], k_msk[:, cs]).then_inc(s_k1, 1)
                if q > 0:
                    cs = slice(512 * (q - 1), 512 * q)
                    act.wait_ge(s_rq, q)
                    nc.scalar.copy(q_p[:, 1, cs], q_rest[:, cs]).then_inc(s_q2, 1)
                    act.wait_ge(s_rk, q)
                    nc.scalar.copy(k_p[:, 1, cs], k_rest[:, cs]).then_inc(s_k2, 1)
            for q in range(4):
                act.wait_ge(s_vproj, q + 1)
                nc.scalar.copy(v_all[:, :, 4 * q:4 * q + 4, 0:DH],
                               spare[q][:, :].rearrange("p (g h d) -> p h g d", g=4, h=H)).then_inc(s_v, 1)

            def slot(it, r):
                e, b = divmod(r, OCT)
                o, S = 2 * it + e, ITER * it + r
                gru = live(S, STEPS)
                if isinstance(o, int) and o == -LEAD_MAX and b % 2 == 1:
                    q = b // 2
                    act.wait_ge(s_turned, q + 1)
                    nc.scalar.copy(xT[:, :, :, 2 * q:2 * q + 2].rearrange("p i c b -> p b i c"),
                                   spare[q][:, :].rearrange("p (b i c) -> p b i c", b=2, i=NI)).then_inc(s_xt, 1)
                if gru:
                    act.wait_ge(rn_done, S + 1)
                    nc.scalar.activation(tr[:, :], bN[:, 0:W64], ACT.Tanh, scale=0.5).then_inc(tr_done, 1)
                    act.wait_ge(z_done, S + 1)
                    nc.scalar.activation(tz[:, :], bZ[:, 0:W64], ACT.Tanh, scale=0.5).then_inc(tz_done, 1)
                for g, slot_ev in ((0, 6), (1, 2)):
                    hy = o + LEAD_EXP - g
                    if b == slot_ev and live(hy, H):
                        act.wait_ge(pv_done, 2 * hy + g + 1)
                        at_least(act, yt_done, 2 * hy + g)
                        nc.scalar.copy(yT[:, :], bPV[:, 0:T]).then_inc(yT_done, 1)
                hm = o + LEAD_ROW
                if b == rows_slot(o) + 1 and live(hm, H):
                    act.wait_ge(mxT_done, hm + 1)
                    at_least(act, st_shift[(e + LEAD_ROW + 1) % 2], 16 * (it + (e + LEAD_ROW + 1) // 2))
                    nc.scalar.copy(mx_rows[:, :], bX[:, :].bitcast(BF16)[0:3 * B * NI, 0:128]).then_inc(mxrow_done, 1)
                if b == 4 and live(o - 1, H):
                    rows_out(o - 1, (e + 1) % 2, it - 1 + e)
                gp = it + 1
                if gru:
                    act.wait_ge(npre_done, S + 1)
                    nc.scalar.activation(h_mul[:, :, 1].rearrange("p (i b) -> p i b", i=NI), n_pre[:, :, :],
                                         ACT.Tanh).then_inc(nt_done, 1)
                if r == ITER - 1 and live(gp, STEPS // ITER):
                    act.wait_ge(gin_mm_done, gp + 1)
                    at_least(act, npre_done, ITER * gp)
                    if isinstance(it, int) and it == -1:
                        act.wait_ge(l_bias, 16 * (2 + NJ))
                    for i in range(NI):
                        nc.scalar.activation(gin_cur[:, i, :, :].rearrange("p s b -> p (s b)"), bGn[:, 128 * i:128 * (i + 1)],
                                             ACT.Identity, bias=bias_n[:, i:i + 1]).then_inc(gin_done, 1)
                hp = o + LEAD_EXP
                if live(hp, H):
                    g, jj = divmod(b, GRP)
                    act.wait_ge(s2_done, B * hp + b + 1)
                    if jj == 0:
                        at_least(act, pv_done, 2 * (hp - 1) + g + 1)
                    nc.scalar.activation(probs[:, g, jj, :], score_bank(S, b % 2, bS2, bZ)[:, :], ACT.Exp, scale=SCALE).then_inc(exp_done, 1)

            def rows_out(o, par, before):
                act.wait_ge(outT_done, o + 1)
                at_least(act, st_out[par], 16 * before)
                nc.scalar.copy(o_sb[:, par, :].rearrange("p (j i f) -> p i j f", j=NJ, i=NI),
                               bGn[:, T:2 * T].rearrange("p (i j f) -> p i j f", i=NI, j=NJ)).then_inc(outev_done, 1)

            slots(act, slot)

        @block.vector
        def _(dve):
            dve.memset(h0[:, :], 0.0).then_inc(s_h0z, 1)
            dve.memset(k_stk[0:ROW_T, :, :].bitcast(F32), 0.0).then_inc(s_kfill, 1)
            dve.wait_ge(l_mask8, 32)
            chain = [0]

            def link(ins):
                chain[0] += 1
                ins.then_inc(s_mrow, 1)
                dve.wait_ge(s_mrow, chain[0])

            link(dve.tensor_scalar(m8[:, 0, :], mask8[:, :], 1.0, -NEG, ALU.subtract, ALU.mult))
            link(dve.tensor_reduce(m8s[:, 1:2], m8[:, 0, :], AX.X, ALU.max))
            link(dve.tensor_scalar(m8s[:, 2:3], m8s[:, 0:1], 1.0 / SCALE, None, ALU.mult))
            link(dve.tensor_scalar(m8[:, 1, :], m8[:, 0, :], m8s[:, 1:2], None, ALU.subtract))
            link(dve.scalar_tensor_tensor(out=m8[:, 2, :], in0=mask8[:, :], scalar=m8s[:, 2:3], in1=m8[:, 1, :],
                                          op0=ALU.mult, op1=ALU.add))

            def perm_out(ap):
                return ap.rearrange("p (i j f) -> p i j f", i=NI, j=NJ)

            def perm_in(ap):
                return ap.rearrange("p (j i f) -> p i j f", j=NJ, i=NI)

            link(dve.tensor_copy(perm_out(m8[:, 3, :]), perm_in(m8[:, 2, :])))
            link(dve.tensor_copy(rows8[:, 0, :], m8[:, 3, :]))
            link(dve.tensor_tensor(m8[:, 0, :], m8[:, 3, :], rows8[:, 0, :], ALU.subtract))
            link(dve.tensor_copy(rows8[:, 1, :], m8[:, 0, :]))
            link(dve.tensor_tensor(rows8[:, 2, :], m8[:, 0, :], rows8[:, 1, :], ALU.subtract))
            for k in range(3):
                last = dve.tensor_copy(perm_out(rows8[:, 3 + k, :]), perm_in(mask8[:, :]))
            last.then_inc(s_rows8, 1)

            dve.wait_ge(l_mask, 16)
            for q in range(4):
                cs = slice(512 * q, 512 * (q + 1))
                dve.wait_ge(s_proj, 2 * q + 2)
                for half in range(2):
                    b = 2 * q + half
                    mk = dve.tensor_tensor(perm_out(k_msk[:, T * b:T * (b + 1)]), perm_out((bS2, bZ)[q % 2][:, T * half:T * (half + 1)]),
                                           perm_in(mask_bc[:, T * b:T * (b + 1)]), ALU.mult)
                mk.then_inc(s_km, 1)
                dve.wait_ge(s_q1, q + 1)
                dve.tensor_tensor(q_rest[:, cs], (bS1, bN)[q % 2][:, :], q_p[:, 0, cs], ALU.subtract).then_inc(s_rq, 1)
                dve.wait_ge(s_k1, q + 1)
                dve.tensor_tensor(k_rest[:, cs], k_msk[:, cs], k_p[:, 0, cs], ALU.subtract).then_inc(s_rk, 1)
            for p, rest, second in ((q_p, q_rest, s_q2), (k_p, k_rest, s_k2)):
                dve.wait_ge(second, 4)
                dve.tensor_tensor(p[:, 2, cs], rest[:, cs], p[:, 1, cs], ALU.subtract).then_inc(s_last3, 1)

            def gru_setup():
                dve.wait_ge(l_gw, 16 * 8)
                dve.tensor_scalar(whh[:, :, 2 * T:3 * T], whh[:, :, 2 * T:3 * T], 0.5, None, ALU.mult).then_inc(s_half, 1)
                dve.wait_ge(l_bias, 16 * (2 + NJ))
                bi = bih_bc[:, :].rearrange("p (g j c) -> p g j c", g=3, j=NJ)
                bh = bhh_bc[:, :].rearrange("p (g j c) -> p g j c", g=3, j=NJ)
                bo = bias_gi[:, :, :, :].rearrange("p j g c -> p g j c")
                for g in range(2):
                    dve.tensor_tensor(bo[:, g], bi[:, g], bh[:, g], ALU.add).then_inc(s_bias_gi, 1)
                links = [0]

                def blink(ins):
                    links[0] += 1
                    ins.then_inc(s_bhn, 1)
                    dve.wait_ge(s_bhn, links[0])

                blink(dve.tensor_scalar(bhn_r[:, 0, :], bhh_bc[:, 2 * T:3 * T], 0.5, None, ALU.mult))
                blink(dve.tensor_copy(bhn_p[:, 0, :], bhn_r[:, 0, :]))
                blink(dve.tensor_tensor(bhn_r[:, 1, :], bhn_r[:, 0, :], bhn_p[:, 0, :], ALU.subtract))
                blink(dve.tensor_copy(bhn_p[:, 1, :], bhn_r[:, 1, :]))
                blink(dve.tensor_tensor(bhn_p[:, 2, :], bhn_r[:, 1, :], bhn_p[:, 1, :], ALU.subtract))
                dve.wait_ge(s_ident, 1)
                blink(dve.tensor_scalar(bhn_r[:, 0, :], bhn_p[:, 0, :], ident[:, 0:1], None, ALU.mult))
                blink(dve.scalar_tensor_tensor(out=bhn_r[:, 1, :], in0=bhn_p[:, 1, :], scalar=ident[:, 1:2],
                                               in1=bhn_r[:, 0, :], op0=ALU.mult, op1=ALU.add))
                dve.scalar_tensor_tensor(out=bhn_rows[:, :], in0=bhn_p[:, 2, :], scalar=ident[:, 2:3],
                                         in1=bhn_r[:, 1, :], op0=ALU.mult, op1=ALU.add).then_inc(s_bhn_rows, 1)
                dve.wait_ge(l_h0, 64)
                dve.wait_ge(s_h0z, 1)
                dve.transpose(h0T[:, :, :].rearrange("p i b -> p (i b)"), h0[:, :]).then_inc(s_h0T, 1)
                dve.wait_ge(s_h0T, 1)
                dve.tensor_copy(h_st[:, :, 1].rearrange("p (i b) -> p i b", i=NI), h0T[:, :, 0:B]).then_inc(h_ready, 1)
                dve.wait_ge(s_scan0, 5)

            def slot(it, r):
                e, b = divmod(r, OCT)
                o, S = 2 * it + e, ITER * it + r
                gru = live(S, STEPS)
                if gru:
                    dve.wait_ge(tr_done, S + 1)
                    dve.scalar_tensor_tensor(out=rn[:, :], in0=tr[:, :], scalar=1.0, in1=bN[:, W64:2 * W64],
                                             op0=ALU.add, op1=ALU.mult).then_inc(rn_used, 1)
                    dve.wait_ge(rn_used, S + 1)
                    dve.transpose(rnT[:, :, :].rearrange("p i b -> p (i b)"), rn[:, :]).then_inc(rnT_done, 1)
                    dve.wait_ge(tz_done, S + 1)
                    dve.transpose(tzT[:, :, :].rearrange("p i b -> p (i b)"), tz[:, :]).then_inc(tzT_done, 1)
                    dve.wait_ge(rnT_done, S + 1)
                    if r == 0:
                        at_least(dve, gin_done, 2 * it + 2)
                    dve.tensor_tensor(n_pre[:, :, :], rnT[:, :, 0:B], gin_cur[:, :, r, :], ALU.add).then_inc(npre_done, 1)
                    dve.wait_ge(tzT_done, S + 1)
                    dve.wait_ge(hh_done, S + 1)
                    dve.scalar_tensor_tensor(out=h_add[:, :, 1].rearrange("p (i b) -> p i b", i=NI), in0=tzT[:, :, 0:B], scalar=1.0,
                                             in1=hh[:, :].rearrange("p (i b) -> p i b", i=NI),
                                             op0=ALU.add, op1=ALU.mult).then_inc(zh_done, 1)
                    dve.tensor_scalar(h_add[:, :, 0].rearrange("p (i b) -> p i b", i=NI), tzT[:, :, 0:B], -0.5, 0.5,
                                      ALU.mult, ALU.add).then_inc(omz_done, 1)
                    if r == ITER - 1 and live(it + 1, STEPS // ITER):
                        gate_inputs(it + 1, 0)
                    dve.wait_ge(nt_done, S + 1)
                    dve.wait_ge(zh_done, S + 1)
                    dve.wait_ge(omz_done, S + 1)
                    at_least(dve, oT_done, S)
                    dve.tensor_tensor_scan(h_st[:, :, :].rearrange("p a e -> p (a e)"), h_mul[:, :, :].rearrange("p a e -> p (a e)"),
                                           h_add[:, :, :].rearrange("p a e -> p (a e)"), 0.0, ALU.mult, ALU.add).then_inc(h_ready, 1)
                elif r == ITER - 1 and live(it + 1, STEPS // ITER):
                    gate_inputs(it + 1, 0)
                if r == ITER - 1 and live(it + 1, STEPS // ITER):
                    gate_inputs(it + 1, 1)
                for g, slot_n in ((0, 0), (1, 3)):
                    hy = o + LEAD_EXP - 1
                    if b == slot_n and live(hy, H):
                        yv = bX[:, 0:T].rearrange("p (i b d) -> p i b d", i=NI, b=GRP)
                        dve.wait_ge(yt_done, 2 * hy + g + 1)
                        at_least(dve, x1_done, 2 * hy + g)
                        dve.reciprocal(y_inv[:, :, :], yv[:, :, :, DH]).then_inc(inv_done, 1)
                        dve.wait_ge(inv_done, 2 * hy + g + 1)
                        dve.tensor_tensor(y_n[:, :, :, :], yv[:, :, :, 0:DH],
                                          y_inv[:, :, :].unsqueeze(3).to_broadcast([128, NI, GRP, DH]),
                                          ALU.mult).then_inc(norm_done, 1)
                hx = o + LEAD_MAX
                if live(hx, H):
                    dve.wait_ge(s1_done, B * hx + b + 1)
                    if b == 0:
                        at_least(dve, split_done, hx - 1)
                    dve.tensor_reduce(neg_max[:, (e + LEAD_MAX) % 2, NI * b:NI * b + NI],
                                      score_bank(S, b % 2, bS1, bN)[:, :].rearrange("p (i k) -> p i k", i=NI), AX.X, ALU.max,
                                      negate=True).then_inc(max_done, 1)

            def gate_inputs(gp, half):
                js = slice(2 * half, 2 * half + 2)
                if half == 0:
                    dve.wait_ge(gimm_done, gp + 1)
                    at_least(dve, sel_done, ITER * gp)
                dve.tensor_tensor(gi_cur[:, js, :], bG[:, 256 * half:256 * (half + 1)].rearrange("p (j c) -> p j c", j=2),
                                  bias_gi[:, js, :, :].rearrange("p j g c -> p j (g c)"), ALU.add).then_inc(gicur_done, 1)

            gru_setup()
            slots(dve, slot)

        @block.tensor
        def _(pe):
            pe.wait_ge(l_w, 48)
            pe.wait_ge(s_ident, 1)
            for n in range(3):
                last = nc.tensor.transpose(bX[:, C * n:C * (n + 1)], w_nat[:, n, :], ident[:, :])
            last.then_inc(s_wt, 1)
            pe.wait_ge(s_wT, 1)
            for q in range(4):
                cs = slice(512 * q, 512 * (q + 1))
                pe.wait_ge(s_xp, 2 * (q + 1))
                at_least(pe, s_rq, q - 1)
                nc.tensor.matmul((bS1, bN)[q % 2][:, :], wT[:, 0, :], xp[:, cs], start=True, stop=True).then_inc(s_proj, 1)
                at_least(pe, s_km, q - 1)
                nc.tensor.matmul((bS2, bZ)[q % 2][:, :], wT[:, 1, :], xp[:, cs], start=True, stop=True).then_inc(s_proj, 1)
            for q in range(4):
                for g in range(4):
                    blk = xp[:, 512 * q + 128 * g:512 * q + 128 * (g + 1)]
                    last = nc.tensor.matmul(spare[q][:, 128 * g:128 * (g + 1)], blk, wT[:, 2, :], start=True, stop=True)
                last.then_inc(s_vproj, 1)
            pe.wait_ge(s_sel, 1)
            pe.wait_ge(s_identb, 1)
            pe.wait_ge(s_fill, 5)
            pe.wait_ge(s_scan0, 5)
            pe.wait_ge(s_rq, 4)
            pe.wait_ge(s_km, 4)

            def hidden(bk, first, n):
                for i in range(NI):
                    for j in range(NJ):
                        w = whh[:, i, :].rearrange("p (g j c) -> p j g c", g=3, j=NJ)[:, j, first:first + 2 * n - 1:2]
                        last = nc.tensor.matmul(bk[32 * j:32 * j + B, 0:n * W64], h_st[:, B * i:B * (i + 1), 1], w,
                                                start=False, stop=(i == NI - 1), skip_group_check=True)
                return last

            def given(bk, s, g):
                for j in range(NJ):
                    last = nc.tensor.matmul(bk[32 * j:32 * j + 32, 0:W64], sel[:, s, :],
                                            gi_cur[:, j, W64 * g:W64 * (g + 1)],
                                            start=True, stop=False, skip_group_check=True)
                return last

            def slot(it, r):
                e, b = divmod(r, OCT)
                o, S = 2 * it + e, ITER * it + r
                if live(S, STEPS):
                    pe.wait_ge(h_ready, S + 1)
                    hidden(bN, 0, 2).then_inc(rn_done, 1)
                    hidden(bZ, 1, 1).then_inc(z_done, 1)
                ahead = live(S + 1, STEPS)
                s = (r + 1) % ITER
                if isinstance(it, int) and it == -1 and r == ITER - 1:
                    pe.wait_ge(max_done, B * LEAD_MAX - 1)
                    pe.wait_ge(exp_done, B * LEAD_EXP - 1)
                    pe.wait_ge(s_bhn_rows, 1)
                    pe.wait_ge(s_half, 1)
                hx = o + LEAD_MAX
                if live(hx, H):
                    par = (e + LEAD_MAX) % 2
                    if isinstance(hx, int) and hx == 0 and b == 0:
                        pe.wait_ge(st_first, 96)
                        pe.wait_ge(st_mask, 32)
                    if b == (4 if isinstance(hx, int) and hx == 0 else 0):
                        pe.wait_ge(st1[par], 2 * 16 * (it + (e + LEAD_MAX) // 2 + 1 + 2 * (1 - par)))
                    at_least(pe, max_done, free_below(S, B * hx + b))
                    qs, ks = stk1[par]
                    for i in range(NI):
                        last = nc.tensor.matmul(score_bank(S, b % 2, bS1, bN)[:, T * i:T * (i + 1)], qs[0:ROW_M, T * b + 128 * i:T * b + 128 * (i + 1)],
                                                ks[0:ROW_M, T * b:T * (b + 1)], start=True, stop=True)
                    last.then_inc(s1_done, 1)
                if not live(o + LEAD_EXP, H) and ahead:
                    keep_awake(2)
                if ahead and r < ITER - 1:
                    prepare(it, r, s, S)
                if isinstance(o, int) and o == -LEAD_MAX:
                    turn_x(b)
                hp = o + LEAD_EXP
                if not live(hp, H) and ahead:
                    keep_awake(2)
                if live(hp, H):
                    par = (e + LEAD_EXP) % 2
                    if b == 0:
                        n_th = it + (e + LEAD_EXP) // 2 + 1
                        pe.wait_ge(st2[par], 2 * 16 * n_th)
                        pe.wait_ge(st_shift[par], 16 * n_th)
                    at_least(pe, exp_done, free_below(S, B * hp + b))
                    qs, ks = stk2[par]
                    for i in range(NI):
                        last = nc.tensor.matmul(score_bank(S, b % 2, bS2, bZ)[:, T * i:T * (i + 1)], ks[0:NROW, T * b + 128 * i:T * b + 128 * (i + 1)],
                                                qs[0:NROW, T * b:T * (b + 1)], start=True, stop=True)
                    last.then_inc(s2_done, 1)
                for g, slot_pv, slot_t in ((0, 4, 7), (1, 0, 2)):
                    hy = o + LEAD_EXP - g
                    if b in (slot_pv, slot_pv + 1) and live(hy, H):
                        i = b - slot_pv
                        if i == 0:
                            pe.wait_ge(exp_done, B * hy + GRP * (g + 1))
                            pe.wait_ge(vcur_done, hy + 1)
                            at_least(pe, yT_done, 2 * hy + g)
                        for jj in range(GRP):
                            last = nc.tensor.matmul(bPV[32 * jj:32 * jj + 32, 0:T], v_cur[:, NI * (GRP * g + jj) + i, :],
                                                    probs[:, g, jj, T * i:T * (i + 1)],
                                                    start=(i == 0), stop=(i == NI - 1), skip_group_check=True)
                        if i == NI - 1:
                            last.then_inc(pv_done, 1)
                    if b == slot_t and live(hy, H):
                        pe.wait_ge(yT_done, 2 * hy + g + 1)
                        if g == 0:
                            at_least(pe, mxrow_done, o + LEAD_ROW + 1, H)
                            at_least(pe, norm_done, 2 * hy)
                        else:
                            at_least(pe, norm_done, 2 * hy + 1)
                        for i in range(NI):
                            last = nc.tensor.transpose(bX[:, 128 * i:128 * (i + 1)], yT[:, 128 * i:128 * (i + 1)], ident[:, :])
                        last.then_inc(yt_done, 1)
                hm = o + LEAD_ROW
                if b == rows_slot(o) and live(hm, H):
                    pe.wait_ge(split_done, hm + 1)
                    if isinstance(hm, int) and hm == 0:
                        pe.wait_ge(s_xt, 4)
                    at_least(pe, norm_done, 2 * (o + LEAD_EXP))
                    nc.tensor.transpose(bX[:, :].bitcast(BF16)[:, 0:128],
                                        mx_p[:, :, :].rearrange("p n a -> p (n a)"), identb[:, :]).then_inc(mxT_done, 1)
                gp = it + 1
                if r in (12, 13, 14) and live(gp, STEPS // ITER):
                    if r == 12:
                        at_least(pe, x1cur_done, 4 * (gp + 1))
                        at_least(pe, gicur_done, 2 * gp)
                        if isinstance(it, int) and it == -1:
                            pe.wait_ge(l_gw, 128)
                    for j in ((0,), (1,), (2, 3))[r - 12]:
                        for i in range(NI):
                            last = nc.tensor.matmul(bG[:, 128 * j:128 * (j + 1)], x1_cur[:, i, :, :, :].rearrange("p a c b -> p (a c b)"),
                                                    wih[:, i, :].rearrange("p (g j c) -> p j g c", g=3, j=NJ)[:, j, 0:2],
                                                    start=(i == 0), stop=(i == NI - 1))
                    if r == 14:
                        last.then_inc(gimm_done, 1)
                if r == 15 and live(gp, STEPS // ITER):
                    at_least(pe, gin_done, NI * gp)
                    at_least(pe, outev_done, o)
                    if isinstance(it, int) and it == -1:
                        pe.wait_ge(s_wihn, NI)
                    for io in range(NI):
                        for i in range(NI):
                            last = nc.tensor.matmul(bGn[:, 128 * io:128 * (io + 1)], wih_n[:, i, io, :],
                                                    x1_cur[:, i, :, :, :].rearrange("p a c b -> p (a c b)"),
                                                    start=(i == 0), stop=(i == NI - 1))
                    last.then_inc(gin_mm_done, 1)
                if b == 3 and live(o - 1, H):
                    pe.wait_ge(oT_done, OCT * o)
                    at_least(pe, outev_done, o - 1)
                    at_least(pe, gin_done, NI * (it + 1), NI * (STEPS // ITER))
                    for i in range(NI):
                        last = nc.tensor.transpose(bGn[:, T + 128 * i:T + 128 * (i + 1)], oT[:, (e + 1) % 2, i, :], ident[:, :])
                    last.then_inc(outT_done, 1)
                if ahead and r == ITER - 1:
                    prepare(it, r, s, S)

            def keep_awake(n):
                at_least(pe, max_done, B * H)
                for i in range(n):
                    nc.tensor.matmul(bS1[:, 0:T], stk1[0][0][0:ROW_M, 0:128], stk1[0][1][0:ROW_M, 0:T], start=True, stop=True)

            def turn_x(b):
                q, second = divmod(b, 2)
                pe.wait_ge(s_v, q + 1)
                for g in (2 * second, 2 * second + 1):
                    blk = xp[:, 512 * q + 128 * g:512 * q + 128 * (g + 1)]
                    last = nc.tensor.transpose(spare[q][:, 128 * g:128 * (g + 1)], blk, ident[:, :])
                if second == 1:
                    last.then_inc(s_turned, 1)

            def prepare(it, r, s, S):
                if r == ITER - 1:
                    pe.wait_ge(gicur_done, 2 * (it + 1) + 2)
                at_least(pe, rn_used, S + 1)
                given(bN, s, 0)
                for j in range(NJ):
                    nc.tensor.matmul(bN[32 * j:32 * j + 32, W64:2 * W64], ones_rows[:, :], bhn_rows[:, W64 * j:W64 * (j + 1)],
                                     start=False, stop=False, skip_group_check=True)
                at_least(pe, tz_done, S + 1)
                given(bZ, s, 1).then_inc(sel_done, 1)

            slots(pe, slot)


_INS = ['x', 'cond_2048', 'L0_cond_Wq', 'L0_cond_Wk', 'L0_cond_Wv', 'L0_cond_b',
        'L1_cond_W_ih', 'L1_cond_W_hh', 'L1_cond_b_ih', 'L1_cond_b_hh']


def kernel(**inputs):
    import numpy as np
    import concourse.bacc as bacc
    from concourse.bass_utils import run_bass_kernel_spmd

    nc = bacc.Bacc("TRN2", target_bir_lowering=False, num_devices=1)
    arrays, args = {}, []
    for name in _INS:
        a = np.ascontiguousarray(inputs[name])
        arrays[f"in_{name}"] = a
        args.append(nc.dram_tensor(f"in_{name}", a.shape, mybir.dt.from_np(a.dtype), kind="ExternalInput").ap())
    out = nc.dram_tensor("out_x", [B, C, T], F32, kind="ExternalOutput").ap()
    build(nc, *args, out)
    r = run_bass_kernel_spmd(nc, [arrays], core_ids=[0])
    return r.results[0]["out_x"]
```
